# Optimizing a Trainium2 kernel written in Bass

```python
import numpy as np
import jax
import jax.numpy as jnp

def _softmax(x, axis=-1):
    return jax.nn.softmax(x, axis=axis)

def _gelu(x):
    return jax.nn.gelu(x, approximate=True)

def _silu(x):
    return jax.nn.silu(x)

def _sigmoid(x):
    return jax.nn.sigmoid(x)

def _layernorm(x, axis=-1, eps=1e-05):
    m = jnp.mean(x, axis=axis, keepdims=True)
    v = jnp.var(x, axis=axis, keepdims=True)
    return (x - m) / jnp.sqrt(v + eps)

def _scatter_add(tgt, idx, src, axis=0):
    return tgt.at[idx].add(src)

def _segment_sum(src, seg, n):
    return jax.ops.segment_sum(src, seg, n)
kernel_name = 'mk_conv_seq_d2_conv_nchw256_r2_a24d8c'

def setup_inputs(seed: int=0):
    np.random.seed(seed)
    _w = jnp.asarray

    def _rec_inputs():
        import jax
        import jax.numpy as jnp
        _gk = jax.random.key(seed)
        x = 7.22e-05 + 1 * jax.random.normal(jax.random.fold_in(_gk, 1), (8, 128, 32, 32), jnp.float32)
        return x
    x = _rec_inputs()

    def _L0_conv_setup():
        import jax, jax.numpy as jnp
        import numpy as np
        C = 128

        def _conv1x1(x, w, b):
            return jnp.einsum('oc,bchw->bohw', w, x) + b[None, :, None, None]
        key = jax.random.key(seed)
        ks = jax.random.split(key, 10)
        scale = 1.0 / np.sqrt(C)
        inp = {'x': jax.random.normal(ks[0], (8, C, 32, 32), dtype=jnp.float32), 'theta_w': jax.random.uniform(ks[1], (C, C), jnp.float32, -scale, scale), 'theta_b': jax.random.uniform(ks[2], (C,), jnp.float32, -scale, scale), 'phi_w': jax.random.uniform(ks[3], (C, C), jnp.float32, -scale, scale), 'phi_b': jax.random.uniform(ks[4], (C,), jnp.float32, -scale, scale), 'g_w': jax.random.uniform(ks[5], (C, C), jnp.float32, -scale, scale), 'g_b': jax.random.uniform(ks[6], (C,), jnp.float32, -scale, scale), 'wz_w': jax.random.uniform(ks[7], (C, C), jnp.float32, -scale, scale), 'wz_b': jax.random.uniform(ks[8], (C,), jnp.float32, -scale, scale), 'w': jnp.float32(0.5)}
        return inp
    _L0_conv_all = _L0_conv_setup()
    _L0_conv_in = {k: v for k, v in _L0_conv_all.items() if k in ('theta_w', 'theta_b', 'phi_w', 'phi_b', 'g_w', 'g_b', 'wz_w', 'wz_b', 'w')}
    del _L0_conv_all

    def _L1_conv_setup():
        import jax, jax.numpy as jnp
        import numpy as np
        B, C, H, W = (4, 128, 32, 32)
        CK = C // 8
        key = jax.random.key(seed)
        ks = jax.random.split(key, 9)
        s = 0.02
        return {'x': jax.random.normal(ks[0], (B, C, H, W), dtype=jnp.float32), 'Wq': jax.random.normal(ks[1], (CK, C), dtype=jnp.float32) * s, 'bq': jnp.zeros((CK,), dtype=jnp.float32), 'Wk': jax.random.normal(ks[2], (CK, C), dtype=jnp.float32) * s, 'bk': jnp.zeros((CK,), dtype=jnp.float32), 'Wv': jax.random.normal(ks[3], (C, C), dtype=jnp.float32) * s, 'bv': jnp.zeros((C,), dtype=jnp.float32), 'gamma': jnp.asarray(0.01, dtype=jnp.float32), 'Wf': jax.random.normal(ks[4], (C, 2 * C), dtype=jnp.float32) * s, 'bf': jnp.zeros((C,), dtype=jnp.float32)}
    _L1_conv_all = _L1_conv_setup()
    _L1_conv_in = {k: v for k, v in _L1_conv_all.items() if k in ('Wq', 'bq', 'Wk', 'bk', 'Wv', 'bv', 'gamma', 'Wf', 'bf')}
    del _L1_conv_all
    return {'x': x, 'L0_conv_theta_w': _L0_conv_in['theta_w'], 'L0_conv_theta_b': _L0_conv_in['theta_b'], 'L0_conv_phi_w': _L0_conv_in['phi_w'], 'L0_conv_phi_b': _L0_conv_in['phi_b'], 'L0_conv_g_w': _L0_conv_in['g_w'], 'L0_conv_g_b': _L0_conv_in['g_b'], 'L0_conv_wz_w': _L0_conv_in['wz_w'], 'L0_conv_wz_b': _L0_conv_in['wz_b'], 'L0_conv_w': _L0_conv_in['w'], 'L1_conv_Wq': _L1_conv_in['Wq'], 'L1_conv_bq': _L1_conv_in['bq'], 'L1_conv_Wk': _L1_conv_in['Wk'], 'L1_conv_bk': _L1_conv_in['bk'], 'L1_conv_Wv': _L1_conv_in['Wv'], 'L1_conv_bv': _L1_conv_in['bv'], 'L1_conv_gamma': _L1_conv_in['gamma'], 'L1_conv_Wf': _L1_conv_in['Wf'], 'L1_conv_bf': _L1_conv_in['bf']}

def reference(x, L0_conv_theta_w, L0_conv_theta_b, L0_conv_phi_w, L0_conv_phi_b, L0_conv_g_w, L0_conv_g_b, L0_conv_wz_w, L0_conv_wz_b, L0_conv_w, L1_conv_Wq, L1_conv_bq, L1_conv_Wk, L1_conv_bk, L1_conv_Wv, L1_conv_bv, L1_conv_gamma, L1_conv_Wf, L1_conv_bf):
    import jax
    import jax.numpy as jnp

    def _L0_conv_ref(x, theta_w, theta_b, phi_w, phi_b, g_w, g_b, wz_w, wz_b, w):
        import jax, jax.numpy as jnp
        import numpy as np
        C = 128

        def _conv1x1(x, w, b):
            return jnp.einsum('oc,bchw->bohw', w, x) + b[None, :, None, None]
        B, Ch, H, W = x.shape
        N = H * W
        theta = _conv1x1(x, theta_w, theta_b).reshape(B, Ch, N)
        phi = _conv1x1(x, phi_w, phi_b).reshape(B, Ch, N)
        g = _conv1x1(x, g_w, g_b).reshape(B, Ch, N)
        scores = jnp.einsum('bcn,bcm->bnm', theta, phi)
        attn = jax.nn.softmax(scores, axis=-1)
        y = jnp.einsum('bnm,bcm->bnc', attn, g)
        y = y.reshape(B, Ch, H, W)
        z = (1.0 - w) * x + w * _conv1x1(y, wz_w, wz_b)
        return z

    def _L1_conv_ref(x, Wq, bq, Wk, bk, Wv, bv, gamma, Wf, bf):
        import jax, jax.numpy as jnp
        import numpy as np
        B, C, H, W = (4, 128, 32, 32)
        CK = C // 8
        b, c, h, w = x.shape
        n = h * w
        xf = x.reshape(b, c, n)
        q = jnp.einsum('oc,bcn->bon', Wq, xf) + bq[None, :, None]
        k = jnp.einsum('oc,bcn->bon', Wk, xf) + bk[None, :, None]
        v = jnp.einsum('oc,bcn->bon', Wv, xf) + bv[None, :, None]
        d_k = q.shape[1]
        att = jnp.einsum('bdi,bdj->bij', q, k) / jnp.sqrt(jnp.asarray(d_k, x.dtype))
        att = jax.nn.softmax(att, axis=-1)
        out = jnp.einsum('bcj,bij->bci', v, att).reshape(b, c, h, w)
        out = gamma * out
        cat = jnp.concatenate([out, x], axis=1)
        fused = jnp.einsum('oc,bchw->bohw', Wf, cat) + bf[None, :, None, None]
        return fused

    def _gn(v, G=32, eps=1e-05):
        B_, C_, H_, W_ = v.shape
        g = v.reshape(B_, G, C_ // G, H_, W_)
        m = jnp.mean(g, axis=(2, 3, 4), keepdims=True)
        s = jnp.var(g, axis=(2, 3, 4), keepdims=True)
        return ((g - m) / jnp.sqrt(s + eps)).reshape(v.shape)

    def _ln_c(v, eps=1e-06):
        m = jnp.mean(v, axis=1, keepdims=True)
        s = jnp.var(v, axis=1, keepdims=True)
        return (v - m) / jnp.sqrt(s + eps)

    def _ln_t(v, eps=1e-05):
        m = jnp.mean(v, axis=-1, keepdims=True)
        s = jnp.var(v, axis=-1, keepdims=True)
        return (v - m) / jnp.sqrt(s + eps)

    def _to_tokens(v):
        B_, C_, H_, W_ = v.shape
        return v.reshape(B_, C_, H_ * W_).transpose(0, 2, 1)

    def _from_tokens(t, like):
        B_, C_, H_, W_ = like.shape
        return t.transpose(0, 2, 1).reshape(B_, C_, H_, W_)
    x = _L0_conv_ref(x, L0_conv_theta_w, L0_conv_theta_b, L0_conv_phi_w, L0_conv_phi_b, L0_conv_g_w, L0_conv_g_b, L0_conv_wz_w, L0_conv_wz_b, L0_conv_w)
    x = _L1_conv_ref(x, L1_conv_Wq, L1_conv_bq, L1_conv_Wk, L1_conv_bk, L1_conv_Wv, L1_conv_bv, L1_conv_gamma, L1_conv_Wf, L1_conv_bf)
    return x

_drawn_inputs = setup_inputs


def setup_inputs(seed=0):
    import zlib

    import numpy as np

    out = dict(_drawn_inputs(seed))
    spreads = {'L1_conv_bq': (0.0, 2.0),
     'L1_conv_bk': (0.0, 2.0),
     'L1_conv_bv': (0.0, 2.0),
     'L1_conv_bf': (0.0, 0.1)}
    factors = {'L0_conv_phi_b': 64.0, 'L1_conv_Wq': 64.0, 'L1_conv_Wk': 64.0, 'L1_conv_Wv': 64.0}
    for name, (base, spread) in spreads.items():
        noise = np.random.default_rng([zlib.crc32(name.encode()), seed]).standard_normal(out[name].shape)
        drawn = base * np.exp(spread * noise) if base else spread * noise
        out[name] = jnp.asarray(drawn.astype(out[name].dtype))
    for name, factor in factors.items():
        out[name] = (out[name] * factor).astype(out[name].dtype)
    return out
```

```python
from contextlib import ExitStack

import concourse.bass as bass
from concourse import mybir

B, C, N, CK = 8, 128, 1024, 16
P = 128
HALF = N // 2
TPB = HALF // P
KT = N // P
CPB = 4
ROW = 32
KROWS = 3 * ROW

BLOCKS = []
for _i in range(B + 2):
    if _i < B:
        BLOCKS.append((0, _i, 0))
    if 0 <= _i - 2:
        BLOCKS.append((1, _i - 2, 1))
    if _i < B:
        BLOCKS.append((0, _i, 1))
    if 0 <= _i - 1 < B:
        BLOCKS.append((1, _i - 1, 0))
UNITS = TPB * len(BLOCKS)
PERIOD = 16
LOOP_FROM, LOOP_TRIPS = 20, 5
LOOP_TO = LOOP_FROM + PERIOD * LOOP_TRIPS
LAST_STEP = UNITS + 7


def block_index(layer, b, h):
    return BLOCKS.index((layer, b, h))


def _schedule():
    at = {k: ([], []) for k in range(-1, LAST_STEP)}

    def put(k, when, *groups):
        at[k][when].extend(groups)

    put(-1, 0, ("theta", 0, 0), ("theta", 0, 1), ("phi", 0, 0), ("phi", 0, 1), ("setup", 0, 0))
    put(0, 0, ("g", 0, 0))
    put(1, 0, ("g", 0, 1))
    put(7, 1, ("theta", 1, 0), ("theta", 1, 1), ("phi", 1, 0), ("phi", 1, 1))
    put(10, 1, ("y", 0, 0))
    put(12, 0, ("z", 0, 0))
    put(13, 1, ("g", 1, 0), ("g", 1, 1))
    put(14, 1, ("y", 0, 1))
    put(15, 1, ("z", 0, 1), ("k", 0, 0), ("k", 0, 1), ("q", 0, 0))
    put(16, 0, ("theta", 2, 0), ("q", 0, 1))
    put(17, 0, ("theta", 2, 1), ("f", 0, 0))
    put(18, 0, ("phi", 2, 0), ("v", 0, 0))
    put(19, 0, ("phi", 2, 1), ("v", 0, 1), ("f", 0, 1))
    for i in range(2, B):
        k = LOOP_FROM + PERIOD * (i - 2)
        put(k, 0, ("y", i - 1, 0))
        put(k + 1, 1, ("z", i - 1, 0))
        put(k + 2, 0, ("g", i, 0))
        put(k + 3, 0, ("y", i - 1, 1), ("g", i, 1))
        put(k + 4, 1, ("z", i - 1, 1))
        put(k + 5, 0, ("r", i - 2, 0))
        put(k + 7, 1, ("k", i - 1, 0))
        put(k + 8, 0, ("k", i - 1, 1), ("q", i - 1, 0))
        put(k + 9, 0, ("f", i - 1, 0))
        put(k + 10, 0, ("q", i - 1, 1))
        if i + 1 < B:
            put(k + 11, 1, ("theta", i + 1, 0))
            put(k + 12, 0, ("theta", i + 1, 1), ("phi", i + 1, 0))
            put(k + 13, 0, ("phi", i + 1, 1))
        put(k + 13, 1, ("r", i - 2, 1))
        put(k + 14, 0, ("v", i - 1, 0))
        put(k + 15, 0, ("v", i - 1, 1), ("f", i - 1, 1))
    t = LOOP_FROM + PERIOD * (B - 2)
    put(t, 0, ("y", B - 1, 0))
    put(t + 1, 1, ("z", B - 1, 0))
    put(t + 2, 1, ("y", B - 1, 1))
    put(t + 3, 1, ("z", B - 1, 1), ("k", B - 1, 0), ("k", B - 1, 1), ("q", B - 1, 0))
    put(t + 4, 0, ("q", B - 1, 1))
    put(t + 5, 0, ("r", B - 2, 0))
    put(t + 7, 0, ("f", B - 1, 0))
    put(t + 8, 0, ("r", B - 2, 1))
    put(t + 9, 1, ("v", B - 1, 0), ("v", B - 1, 1))
    put(t + 11, 0, ("f", B - 1, 1))
    put(t + 12, 0, ("r", B - 1, 0))
    put(t + 16, 0, ("r", B - 1, 1))
    return at


SCHEDULE = _schedule()
ORDER = {}
for _k in range(-1, LAST_STEP):
    for _g in SCHEDULE[_k][0] + SCHEDULE[_k][1]:
        ORDER[_g] = len(ORDER)
GROUPS_PER_PERIOD = sum(len(SCHEDULE[k][0] + SCHEDULE[k][1]) for k in range(LOOP_FROM, LOOP_FROM + PERIOD))

SPLIT_X = {-1: 0, 2: 1, 14: 2, **{LOOP_FROM + PERIOD * (i - 2) + 9: i + 1 for i in range(2, B - 1)}}
KEEP_X = {-1: 0, 2: 1, **{LOOP_FROM + PERIOD * (i - 2) + 6: i for i in range(2, B)}}
LOAD_X = {-1: 0, 0: 1, 3: 2, **{LOOP_FROM + PERIOD * (i - 2) + 7: i + 1 for i in range(2, B - 1)}}

W_THETA, W_PHI, W_G, W_Z, W_F2, W_F1, W_V, W_Q = range(0, 8 * P, P)
W_K = W_Q + CK
W_COLS = 7 * P + 2 * CK
SPLIT_COLS = 5 * P


def build(nc, x, weights_t, columns, qk_bias, g_bias, gates, out):
    f32, f32r = mybir.dt.float32, mybir.dt.float32r
    ALU, ACT, AX = mybir.AluOpType, mybir.ActivationFunctionType, mybir.AxisListType

    with ExitStack() as ctx:
        def sb(name, shape, dt=f32):
            return ctx.enter_context(nc.sbuf_tensor(name, shape, dt))

        def sem(name):
            return ctx.enter_context(nc.semaphore(name))

        w_all = sb("w_all", [P, W_COLS])
        w_hi = sb("w_hi", [P, SPLIT_COLS], f32r)
        w_lo = sb("w_lo", [P, SPLIT_COLS], f32r)
        wqk = sb("wqk", [P, 2, 3, ROW])
        wqk_hi = sb("wqk_hi", [P, 2, KROWS], f32r)
        wqk_lo = sb("wqk_lo", [P, 2, KROWS], f32r)
        wv = sb("wv", [P, P])
        wv_hi = sb("wv_hi", [P, P], f32r)
        wv_lo = sb("wv_lo", [P, P], f32r)
        v_bias = sb("v_bias", [P, P])
        g_bias_rows = sb("g_bias_rows", [P, P])
        bv_cols = sb("bv_cols", [P, P])
        col = sb("col", [P, 5])
        qk_b = sb("qk_b", [P, 2])
        gate = sb("gate", [P, 2])
        keep = sb("keep", [P, 2])
        ident = sb("ident", [P, P])
        ones = sb("ones", [P, P])
        ones_r = sb("ones_r", [P, P], f32r)
        zero = sb("zero", [P, 1])
        warm = sb("warm", [P, 1])

        x_raw = sb("x_raw", [P, N])
        x_hi = sb("x_hi", [P, N], f32r)
        x_lo = sb("x_lo", [P, N], f32r)
        x_keep_0 = sb("x_keep_0", [P, N])
        x_keep = sb("x_keep", [P, N])
        theta_hi = sb("theta_hi", [P, N], f32r)
        theta_lo = sb("theta_lo", [P, N], f32r)
        phi_hi = sb("phi_hi", [P, N], f32r)
        phi_lo = sb("phi_lo", [P, N], f32r)
        g_full = sb("g_full", [P, HALF])
        g_hi = sb("g_hi", [P, N], f32r)
        g_lo = sb("g_lo", [P, N], f32r)
        v_full = sb("v_full", [P, HALF])
        v_hi = sb("v_hi", [P, N], f32r)
        v_lo = sb("v_lo", [P, N], f32r)
        q_op = sb("q_op", [KROWS, N], f32r)
        k_op = sb("k_op", [KROWS, N], f32r)
        probs = sb("probs", [P, 2, N])
        pt_hi = sb("pt_hi", [P, 2, KT, HALF], f32r)
        pt_lo = sb("pt_lo", [P, 2, KT, HALF], f32r)
        neg_max = sb("neg_max", [P, 4])
        row_sum = sb("row_sum", [P, 4, TPB])
        r_inv = sb("r_inv", [P, 4, TPB])
        r_hi = sb("r_hi", [P, TPB], f32r)
        r_lo = sb("r_lo", [P, TPB])
        diag_hi = sb("diag_hi", [P, HALF], f32r)
        diag_lo = sb("diag_lo", [P, HALF], f32r)
        r_rows = sb("r_rows", [P, HALF])
        ut = sb("ut", [P, 2, HALF])
        y_full = sb("y_full", [P, HALF])
        y_hi = sb("y_hi", [P, HALF], f32r)
        y_lo = sb("y_lo", [P, HALF], f32r)
        z_full = sb("z_full", [P, HALF])
        z_hi = sb("z_hi", [P, N], f32r)
        z_lo = sb("z_lo", [P, N], f32r)
        f_part = sb("f_part", [P, N])
        o_sb = sb("o_sb", [P, N])

        scores = ctx.enter_context(nc.psum_tensor("scores", [P, 2, N], f32))
        trans = ctx.enter_context(nc.psum_tensor("trans", [P, N], f32))
        accum = ctx.enter_context(nc.psum_tensor("accum", [P, HALF], f32))
        misc = ctx.enter_context(nc.psum_tensor("misc", [P, HALF], f32))

        weights_loaded = sem("weights_loaded")
        rest_loaded = sem("rest_loaded")
        small_loaded = sem("small_loaded")
        x_loaded = sem("x_loaded")
        ident_ready = sem("ident_ready")
        consts_ready = sem("consts_ready")
        zero_ready = sem("zero_ready")
        w_split = sem("w_split")
        wqk_made = sem("wqk_made")
        wqk_split = sem("wqk_split")
        setup_done = sem("setup_done")
        wv_split = sem("wv_split")
        x_split = sem("x_split")
        x_kept = sem("x_kept")
        scores_ready = sem("scores_ready")
        max_ready = sem("max_ready")
        probs_ready = sem("probs_ready")
        trans_ready = sem("trans_ready")
        pt_hi_ready = sem("pt_hi_ready")
        pt_lo_ready = sem("pt_lo_ready")
        pv_done = sem("pv_done")
        accum_drained = sem("accum_drained")
        r_inv_ready = sem("r_inv_ready")
        misc_ready = sem("misc_ready")
        misc_drained = sem("misc_drained")
        op_hi_ready = sem("op_hi_ready")
        r_split = sem("r_split")
        keep_made = sem("keep_made")
        diag_ready = sem("diag_ready")
        g_split = sem("g_split")
        v_split = sem("v_split")
        y_split = sem("y_split")
        z_split = sem("z_split")
        out_ready = sem("out_ready")
        stored = [sem("stored_0"), sem("stored_1")]

        def units(k, it):
            return k + 1 + PERIOD * it

        def banks(k, bank, it):
            return 2 * k + bank + 1 + 2 * PERIOD * it

        def blocks(gb, it):
            return gb + 1 + (PERIOD // TPB) * it

        def chunks(gb, c, it):
            return CPB * gb + c + 1 + PERIOD * it

        def groups(group, it):
            return ORDER[group] + 1 + GROUPS_PER_PERIOD * it

        def halves(b, h, it, each=1):
            return each * (2 * b + h + 1) + 2 * each * it

        def ops(kind, b, h, it):
            kinds = ("theta", "phi", "q", "k")
            before = [g for g in ORDER if g[0] in kinds and ORDER[g] <= ORDER[(kind, b, h)]]
            return len(before) + 8 * it

        def out_count(gb, it):
            return sum(1 for n in range(gb + 1) if BLOCKS[n][0] == 1) + 2 * it

        def cols(h):
            return slice(h * HALF, (h + 1) * HALF)

        def f(ap):
            return ap.bitcast(f32)

        def steps(engine, emit):
            for k in range(-1, LOOP_FROM):
                emit(k, 0)
            with engine.Fori(0, LOOP_TRIPS) as it:
                for k in range(LOOP_FROM, LOOP_FROM + PERIOD):
                    emit(k, it)
            for k in range(LOOP_TO, LAST_STEP):
                emit(k, 0)

        def slot(gb):
            layer, _, h = BLOCKS[gb]
            return 2 * layer + h

        def last_of_slot(gb):
            layer, b, h = BLOCKS[gb]
            return block_index(layer, b - 1, h) if b else gb - PERIOD // TPB

        def drained_block(k):
            gb, off = divmod(k - 10, TPB)
            return gb if off == 0 and 0 <= gb < len(BLOCKS) else None

        def summed_block(k):
            gb, off = divmod(k - 5, TPB)
            return gb if off == 0 and 0 <= gb < len(BLOCKS) else None

        block = ctx.enter_context(nc.Block())

        @block.sync
        def _(sp):
            sp.dma_start(x_raw[:, :], x[0]).then_inc(x_loaded, 16)
            sp.dma_start(col[:, :], columns).then_inc(small_loaded, 16)
            sp.dma_start(qk_b[:, :], qk_bias).then_inc(small_loaded, 16)
            sp.dma_start(gate[:, :], gates.partition_broadcast(P)).then_inc(small_loaded, 16)
            sp.dma_start(g_bias_rows[:, :], g_bias.partition_broadcast(P)).then_inc(small_loaded, 16)

            def emit(k, it):
                if k in LOAD_X and k >= 0:
                    b = LOAD_X[k]
                    sp.wait_ge(x_kept, b + it)
                    sp.dma_start(x_raw[:, :], x[b + it]).then_inc(x_loaded, 16)
                gb = drained_block(k)
                if gb is not None and BLOCKS[gb][0] == 1:
                    _, b, h = BLOCKS[gb]
                    sp.wait_ge(out_ready, out_count(gb, it))
                    sp.dma_start(out[b + it, :, cols(h)], o_sb[:, cols(h)]).then_inc(stored[h], 16)
            steps(sp, emit)
            for h in range(2):
                sp.wait_ge(stored[h], 16 * B)

        @block.tensor
        def _(pe):
            def three(dst, hi_l, lo_l, hi_r, lo_r):
                nc.tensor.matmul(dst, hi_l, hi_r, start=True, stop=False)
                nc.tensor.matmul(dst, hi_l, lo_r, start=False, stop=False)
                return nc.tensor.matmul(dst, lo_l, hi_r, start=False, stop=True)

            def unit_scores(k, it):
                layer, b, h = BLOCKS[k // TPB]
                t = k % TPB
                if k >= 2:
                    pe.wait_ge(probs_ready, units(k - 2, it))
                if t == 0 and layer == 0:
                    pe.wait_ge(misc_drained, groups(("phi", b, 1), it))
                if t == 0 and layer == 1:
                    pe.wait_ge(misc_drained, groups(("q", b, 0) if h == 0 else ("q", b, 1), it))
                for half in range(2):
                    dst = scores[:, k % 2, cols(half)]
                    if layer == 0:
                        queries = slice(TPB * h + t, N, KT)
                        last = three(dst, theta_hi[:, queries], theta_lo[:, queries],
                                     phi_hi[:, cols(half)], phi_lo[:, cols(half)])
                    else:
                        q0 = h * HALF + t * P
                        last = nc.tensor.matmul(dst, q_op[:, q0:q0 + P], k_op[:, cols(half)], start=True, stop=True)
                last.then_inc(scores_ready, 1)

            def unit_transposes(k, it):
                pe.wait_ge(probs_ready, units(k, it))
                for bank in range(2):
                    if k >= 1:
                        pe.wait_ge(pt_lo_ready, banks(k - 1, bank, it))
                    for n in range(4 * bank, 4 * bank + 4):
                        last = nc.tensor.transpose(trans[:, n * P:(n + 1) * P], probs[:, k % 2, n * P:(n + 1) * P],
                                                   ident[:, :])
                    last.then_inc(trans_ready, 1)

            def value_chunk(gb, c, it):
                layer, b, h = BLOCKS[gb]
                hi, lo = (g_hi, g_lo) if layer == 0 else (v_hi, v_lo)
                if c == 0:
                    pe.wait_ge(pt_lo_ready, banks(TPB * gb + TPB - 1, 1, it))
                    pe.wait_ge(g_split if layer == 0 else v_split, halves(b, 1, it, 2))
                    if gb:
                        pe.wait_ge(accum_drained, blocks(gb - 1, it))
                for n in range(2 * c, 2 * c + 2):
                    tile = slice(n * P, (n + 1) * P)
                    p_hi, p_lo = pt_hi[:, gb % 2, n, :], pt_lo[:, gb % 2, n, :]
                    nc.tensor.matmul(accum[:, :], hi[:, tile], p_hi, start=(n == 0), stop=False)
                    nc.tensor.matmul(accum[:, :], hi[:, tile], p_lo, start=False, stop=False)
                    last = nc.tensor.matmul(accum[:, :], lo[:, tile], p_hi, start=False, stop=(n == KT - 1))
                last.then_inc(pv_done, 1)

            def small(group, it):
                kind, b, h = group
                if ORDER[group]:
                    pe.wait_ge(misc_drained, ORDER[group] + GROUPS_PER_PERIOD * it)
                if kind in ("theta", "phi"):
                    w0 = W_THETA if kind == "theta" else W_PHI
                    pe.wait_ge(x_split, 2 * (b + 1) + 2 * it)
                    last = three(misc[:, :], w_hi[:, w0:w0 + P], w_lo[:, w0:w0 + P], x_hi[:, cols(h)], x_lo[:, cols(h)])
                elif kind in ("g", "v"):
                    if kind == "g":
                        pe.wait_ge(x_split, 2 * (b + 1) + 2 * it)
                        m_hi, m_lo, r_h, r_l = x_hi, x_lo, w_hi[:, W_G:W_G + P], w_lo[:, W_G:W_G + P]
                    else:
                        pe.wait_ge(z_split, halves(b, h, it, 2))
                        m_hi, m_lo, r_h, r_l = z_hi, z_lo, wv_hi[:, :], wv_lo[:, :]
                    for n in range(4):
                        tile = slice(h * HALF + n * P, h * HALF + (n + 1) * P)
                        last = three(misc[:, n * P:(n + 1) * P], m_hi[:, tile], m_lo[:, tile], r_h, r_l)
                elif kind == "y":
                    pe.wait_ge(accum_drained, blocks(block_index(0, b, h), it))
                    for n in range(4):
                        last = nc.tensor.transpose(misc[:, n * P:(n + 1) * P], ut[:, h, n * P:(n + 1) * P], ident[:, :])
                elif kind == "z":
                    pe.wait_ge(y_split, halves(b, h, it, 2))
                    last = three(misc[:, :], w_hi[:, W_Z:W_Z + P], w_lo[:, W_Z:W_Z + P], y_hi[:, :], y_lo[:, :])
                elif kind in ("q", "k"):
                    i = 0 if kind == "q" else 1
                    pe.wait_ge(z_split, halves(b, h, it, 2))
                    last = three(misc[0:KROWS, :], wqk_hi[:, i, :], wqk_lo[:, i, :], z_hi[:, cols(h)], z_lo[:, cols(h)])
                elif kind == "f":
                    last = three(misc[:, :], w_hi[:, W_F2:W_F2 + P], w_lo[:, W_F2:W_F2 + P],
                                 z_hi[:, cols(h)], z_lo[:, cols(h)])
                elif kind == "r":
                    pe.wait_ge(diag_ready, 2 * out_count(block_index(1, b, h), it))
                    nc.tensor.matmul(misc[:, :], ones_r[:, :], diag_hi[:, :], start=True, stop=False)
                    last = nc.tensor.matmul(misc[:, :], ones_r[:, :], diag_lo[:, :], start=False, stop=True)
                else:
                    pe.wait_ge(consts_ready, 4)
                    nc.tensor.matmul(misc[:, 0:P], w_all[:, W_V:W_V + P], w_all[:, W_F1:W_F1 + P], start=True, stop=True)
                    last = nc.tensor.matmul(misc[:, P:2 * P], bv_cols[:, :], w_all[:, W_F1:W_F1 + P],
                                            start=True, stop=True)
                last.then_inc(misc_ready, 1)

            pe.wait_ge(w_split, 2)

            def emit(k, it):
                if 0 <= k < UNITS:
                    unit_scores(k, it)
                if k == 0:
                    pe.wait_ge(w_split, 4)
                    pe.wait_ge(ident_ready, 2)
                if k == 15:
                    pe.wait_ge(wqk_split, 2)
                if k == 18:
                    pe.wait_ge(wv_split, 2)
                before, after = SCHEDULE[k]
                for group in before:
                    small(group, it)
                gb, c = divmod(k - 6, CPB)
                if 0 <= gb < len(BLOCKS):
                    value_chunk(gb, c, it)
                for group in after:
                    small(group, it)
                if 0 <= k - 1 < UNITS:
                    unit_transposes(k - 1, it)
            steps(pe, emit)

        @block.scalar
        def _(act):
            act.dma_start(w_all[:, 0:2 * P], weights_t[:, 0:2 * P]).then_inc(weights_loaded, 16)
            act.dma_start(w_all[:, 2 * P:W_COLS], weights_t[:, 2 * P:W_COLS]).then_inc(rest_loaded, 16)
            act.wait_ge(consts_ready, 1)
            nc.scalar.activation(warm[:, :], ones[:, 0:1], ACT.Exp)
            act.wait_ge(small_loaded, 64)

            def unit_exp(k, it):
                gb, t = divmod(k, TPB)
                act.wait_ge(max_ready, units(k, it))
                if k >= 2:
                    act.wait_ge(trans_ready, banks(k - 2, 1, it))
                if t == 0 and gb >= 5:
                    act.wait_ge(r_inv_ready, blocks(last_of_slot(gb), it))
                nc.scalar.activation(probs[:, k % 2, :], scores[:, k % 2, :], ACT.Exp, bias=neg_max[:, k % 4:k % 4 + 1],
                                     accum_out=row_sum[:, slot(gb), t:t + 1]).then_inc(probs_ready, 1)

            def unit_hi(k, it):
                gb, t = divmod(k, TPB)
                for bank in range(2):
                    act.wait_ge(trans_ready, banks(k, bank, it))
                    if t == 0 and bank == 0 and gb >= 2:
                        act.wait_ge(pv_done, chunks(gb - 2, CPB - 1, it))
                    nc.scalar.activation(pt_hi[:, gb % 2, 4 * bank:4 * bank + 4, t * P:(t + 1) * P],
                                         trans[:, cols(bank)].rearrange("p (n q) -> p n q", n=4),
                                         ACT.Copy).then_inc(pt_hi_ready, 1)

            def small(group, it):
                kind, b, h = group
                if kind not in ("theta", "phi", "q", "k", "f", "r"):
                    return
                act.wait_ge(misc_ready, groups(group, it))
                if kind in ("theta", "phi"):
                    dst, c = (theta_hi, 0) if kind == "theta" else (phi_hi, 1)
                    nc.scalar.activation(dst[:, cols(h)], misc[:, :], ACT.Identity,
                                         bias=col[:, c:c + 1]).then_inc(op_hi_ready, 1)
                elif kind in ("q", "k"):
                    dst, c = (q_op, 0) if kind == "q" else (k_op, 1)
                    nc.scalar.activation(dst[:, cols(h)], misc[0:KROWS, :], ACT.Identity,
                                         bias=qk_b[0:KROWS, c:c + 1]).then_inc(op_hi_ready, 1)
                elif kind == "f":
                    if b > 0:
                        act.wait_ge(out_ready, out_count(block_index(1, b - 1, h), it))
                    nc.scalar.activation(f_part[:, cols(h)], misc[:, :], ACT.Identity,
                                         bias=col[:, 4:5]).then_inc(misc_drained, 1)
                else:
                    nc.scalar.activation(r_rows[:, :], misc[:, :], ACT.Copy).then_inc(misc_drained, 1)

            def keep_x(b, it):
                act.wait_ge(x_split, 2 * b + 2 + 2 * it)
                if b >= 2:
                    act.wait_ge(misc_drained, groups(("z", b - 1, 1), it))
                dst = x_keep_0 if b == 0 else x_keep
                nc.scalar.activation(dst[:, :], x_raw[:, :], ACT.Identity, scale=keep[:, 0:1],
                                     bias=keep[:, 1:2]).then_inc(x_kept, 1)

            def emit(k, it):
                gb = drained_block(k)
                if gb is not None and BLOCKS[gb][0] == 0:
                    _, b, h = BLOCKS[gb]
                    act.wait_ge(pv_done, chunks(gb, CPB - 1, it))
                    if b > 0:
                        act.wait_ge(misc_ready, groups(("y", b - 1, h), it))
                    nc.scalar.activation(ut[:, h, :], accum[:, :], ACT.Copy).then_inc(accum_drained, 1)
                if 0 <= k - 2 < UNITS:
                    unit_hi(k - 2, it)
                if 0 <= k - 1 < UNITS:
                    unit_exp(k - 1, it)
                for group in SCHEDULE[k][0] + SCHEDULE[k][1]:
                    small(group, it)
                if k in KEEP_X:
                    if k < 0:
                        act.wait_ge(keep_made, 2)
                    keep_x(KEEP_X[k], it)
            steps(act, emit)

        @block.vector
        def _(dve):
            nc.vector.memset(ones[:, :], 1.0).then_inc(consts_ready, 1)
            nc.vector.memset(ones_r[:, :].bitcast(f32), 1.0).then_inc(consts_ready, 1)
            nc.vector.memset(wqk[:, :, :, :], 0.0).then_inc(wqk_made, 1)
            dve.wait_ge(weights_loaded, 16)
            nc.vector.tensor_copy(w_hi[:, 0:2 * P], w_all[:, 0:2 * P]).then_inc(w_split, 1)
            dve.wait_ge(w_split, 1)
            nc.vector.tensor_tensor(w_lo[:, 0:2 * P], w_all[:, 0:2 * P], f(w_hi[:, 0:2 * P]),
                                    ALU.subtract).then_inc(w_split, 1)
            dve.wait_ge(small_loaded, 64)

            def late_setup():
                rest = slice(2 * P, SPLIT_COLS)
                dve.wait_ge(rest_loaded, 16)
                nc.vector.tensor_copy(w_hi[:, rest], w_all[:, rest]).then_inc(w_split, 1)
                dve.wait_ge(w_split, 3)
                nc.vector.tensor_tensor(w_lo[:, rest], w_all[:, rest], f(w_hi[:, rest]),
                                        ALU.subtract).then_inc(w_split, 1)
                dve.wait_ge(consts_ready, 2)
                nc.vector.tensor_scalar(bv_cols[:, :], ones[:, :], col[:, 3:4], None, ALU.mult).then_inc(consts_ready, 1)
                nc.vector.tensor_scalar(qk_b[:, 0:1], qk_b[:, 0:1], CK ** -0.5, None, ALU.mult).then_inc(consts_ready, 1)
                dve.wait_ge(wqk_made, 1)
                for i, (w0, scale) in enumerate(((W_Q, CK ** -0.5), (W_K, 1.0))):
                    for n in range(3):
                        nc.vector.tensor_scalar(wqk[:, i, n, 0:CK], w_all[:, w0:w0 + CK], scale, None,
                                                ALU.mult).then_inc(wqk_made, 1)
                dve.wait_ge(wqk_made, 7)
                flat = wqk[:, :, :, :].rearrange("p i n c -> p i (n c)")
                nc.vector.tensor_copy(wqk_hi[:, :, :], flat).then_inc(wqk_split, 1)
                dve.wait_ge(wqk_split, 1)
                nc.vector.tensor_tensor(wqk_lo[:, :, :], flat, f(wqk_hi[:, :, :]), ALU.subtract).then_inc(wqk_split, 1)

            def unit_max(k, it):
                dve.wait_ge(scores_ready, units(k, it))
                if k >= 4:
                    dve.wait_ge(probs_ready, units(k - 4, it))
                nc.vector.tensor_reduce(neg_max[:, k % 4:k % 4 + 1], scores[:, k % 2, :], AX.X, ALU.max,
                                        negate=True).then_inc(max_ready, 1)

            def unit_lo(k, it):
                gb, t = divmod(k, TPB)
                for bank in range(2):
                    dve.wait_ge(pt_hi_ready, banks(k, bank, it))
                    if t == 0 and bank == 0 and gb >= 2:
                        dve.wait_ge(pv_done, chunks(gb - 2, CPB - 1, it))
                    at = (slice(None), gb % 2, slice(4 * bank, 4 * bank + 4), slice(t * P, (t + 1) * P))
                    nc.vector.tensor_tensor(pt_lo[at], trans[:, cols(bank)].rearrange("p (n q) -> p n q", n=4),
                                            f(pt_hi[at]), ALU.subtract).then_inc(pt_lo_ready, 1)

            def small(group, it):
                kind, b, h = group
                if kind in ("f", "r"):
                    return
                if kind in ("theta", "phi", "q", "k"):
                    dve.wait_ge(op_hi_ready, ops(kind, b, h, it))
                    if kind in ("theta", "phi"):
                        (hi, lo), c = ((theta_hi, theta_lo), 0) if kind == "theta" else ((phi_hi, phi_lo), 1)
                        nc.vector.scalar_tensor_tensor(lo[:, cols(h)], misc[:, :], col[:, c:c + 1], f(hi[:, cols(h)]),
                                                       ALU.add, ALU.subtract).then_inc(misc_drained, 1)
                    else:
                        dst, c, r0 = (q_op, 0, ROW) if kind == "q" else (k_op, 1, 2 * ROW)
                        rows = slice(r0, r0 + ROW)
                        nc.vector.scalar_tensor_tensor(dst[rows, cols(h)], misc[rows, :], qk_b[rows, c:c + 1],
                                                       f(dst[rows, cols(h)]), ALU.add,
                                                       ALU.subtract).then_inc(misc_drained, 1)
                    return
                dve.wait_ge(misc_ready, groups(group, it))
                four = misc[:, :].rearrange("p (n c) -> p n c", n=4)
                if kind in ("g", "v"):
                    full, bias, split = (g_full, g_bias_rows, g_split) if kind == "g" else (v_full, v_bias, v_split)
                    if 2 * b + h:
                        dve.wait_ge(split, halves(b, h, it, 2) - 2)
                    if kind == "v" and (b, h) == (0, 0):
                        dve.wait_ge(setup_done, 1)
                    nc.vector.tensor_tensor(full[:, :].rearrange("p (n c) -> p n c", n=4), four,
                                            bias[:, :].unsqueeze(1).broadcast_to([P, 4, P]),
                                            ALU.add).then_inc(misc_drained, 1)
                elif kind == "y":
                    if 2 * b + h:
                        dve.wait_ge(y_split, halves(b, h, it, 2) - 2)
                    gb = block_index(0, b, h)
                    dve.wait_ge(r_inv_ready, blocks(gb, it))
                    nc.vector.tensor_tensor(y_full[:, :].rearrange("p (n c) -> p n c", n=4), four,
                                            r_inv[:, slot(gb), :].unsqueeze(2).broadcast_to([P, 4, P]),
                                            ALU.mult).then_inc(misc_drained, 1)
                elif kind == "z":
                    if 2 * b + h:
                        dve.wait_ge(z_split, halves(b, h, it, 2) - 2)
                    dve.wait_ge(x_kept, b + 1 + it)
                    keep_of = x_keep_0 if b == 0 else x_keep
                    nc.vector.scalar_tensor_tensor(z_full[:, :], misc[:, :], gate[:, 0:1], keep_of[:, cols(h)],
                                                   ALU.mult, ALU.add).then_inc(misc_drained, 1)
                else:
                    nc.vector.tensor_scalar(v_bias[:, :], misc[:, P:2 * P], gate[:, 1:2], None,
                                            ALU.mult).then_inc(setup_done, 1)
                    nc.vector.tensor_scalar(wv[:, :], misc[:, 0:P], gate[:, 1:2], None,
                                            ALU.mult).then_inc(misc_drained, 1)
                    dve.wait_ge(misc_drained, groups(group, it))
                    nc.vector.tensor_copy(wv_hi[:, :], wv[:, :]).then_inc(wv_split, 1)
                    dve.wait_ge(wv_split, 1)
                    nc.vector.tensor_tensor(wv_lo[:, :], wv[:, :], f(wv_hi[:, :]), ALU.subtract).then_inc(wv_split, 1)

            def emit(k, it):
                gb = drained_block(k)
                if gb is not None and BLOCKS[gb][0] == 1:
                    _, b, h = BLOCKS[gb]
                    dve.wait_ge(pv_done, chunks(gb, CPB - 1, it))
                    dve.wait_ge(misc_drained, groups(("r", b, h), it))
                    if b > 0:
                        dve.wait_ge(stored[h], 16 * b + 16 * it)
                    nc.vector.tensor_tensor(o_sb[:, cols(h)], accum[:, :], r_rows[:, :],
                                            ALU.mult).then_inc(accum_drained, 1)
                gb = summed_block(k)
                if gb is not None:
                    dve.wait_ge(probs_ready, units(TPB * gb + TPB - 1, it))
                    nc.vector.reciprocal(r_inv[:, slot(gb), :], row_sum[:, slot(gb), :]).then_inc(r_inv_ready, 1)
                if 0 <= k - 2 < UNITS:
                    unit_lo(k - 2, it)
                for n, group in enumerate(SCHEDULE[k][0]):
                    if group[0] == "setup":
                        late_setup()
                    small(group, it)
                if 0 <= k < UNITS:
                    unit_max(k, it)
                for group in SCHEDULE[k][1]:
                    small(group, it)
            steps(dve, emit)

        @block.gpsimd
        def _(pool):
            nc.gpsimd.memset(zero[:, :], 0.0).then_inc(zero_ready, 1)
            nc.gpsimd.memset(ident[:, :], 0.0).then_inc(ident_ready, 1)
            pool.wait_ge(zero_ready, 1)
            pool.wait_ge(small_loaded, 64)

            def round_to(hi, full):
                return nc.gpsimd.tensor_tensor(hi, full, zero[:, :].broadcast_to([P, full.shape[1]]), ALU.add)

            def split_x(b, it):
                pool.wait_ge(x_loaded, 16 * (b + 1) + 16 * it)
                if b > 0:
                    pool.wait_ge(misc_ready, groups(("g", b - 1, 1), it))
                round_to(x_hi[:, :], x_raw[:, :]).then_inc(x_split, 1)
                pool.wait_ge(x_split, 2 * b + 1 + 2 * it)
                nc.gpsimd.tensor_tensor(x_lo[:, :], x_raw[:, :], f(x_hi[:, :]), ALU.subtract).then_inc(x_split, 1)

            def parts(full, hi, lo, done, count):
                round_to(hi, full).then_inc(done, 1)
                pool.wait_ge(done, count - 1)
                nc.gpsimd.tensor_tensor(lo, full, f(hi), ALU.subtract).then_inc(done, 1)

            def small(group, it):
                kind, b, h = group
                if kind not in ("g", "v", "y", "z"):
                    return
                pool.wait_ge(misc_drained, groups(group, it))
                if kind == "g":
                    if b > 0:
                        pool.wait_ge(pv_done, chunks(block_index(0, b - 1, 1), CPB - 1, it))
                    parts(g_full[:, :], g_hi[:, cols(h)], g_lo[:, cols(h)], g_split, halves(b, h, it, 2))
                elif kind == "v":
                    if b > 0:
                        pool.wait_ge(pv_done, chunks(block_index(1, b - 1, 1), CPB - 1, it))
                    parts(v_full[:, :], v_hi[:, cols(h)], v_lo[:, cols(h)], v_split, halves(b, h, it, 2))
                elif kind == "y":
                    if 2 * b + h:
                        last = ("z", b, 0) if h else ("z", b - 1, 1)
                        pool.wait_ge(misc_ready, groups(last, it))
                    parts(y_full[:, :], y_hi[:, :], y_lo[:, :], y_split, halves(b, h, it, 2))
                else:
                    if b > 0:
                        pool.wait_ge(misc_ready, groups(("f", b - 1, 1), it))
                    parts(z_full[:, :], z_hi[:, cols(h)], z_lo[:, cols(h)], z_split, halves(b, h, it, 2))

            def emit(k, it):
                if k in SPLIT_X:
                    split_x(SPLIT_X[k], it)
                if k == -1:
                    pool.wait_ge(ident_ready, 1)
                    nc.gpsimd.affine_select(out=ident[:, :], in_=ident[:, :], compare_op=ALU.not_equal, fill=1.0, base=0,
                                            pattern=[[-1, P]], channel_multiplier=1).then_inc(ident_ready, 1)
                    nc.gpsimd.tensor_scalar(keep[:, 0:1], gate[:, 0:1], -1.0, 1.0, ALU.mult, ALU.add).then_inc(keep_made, 1)
                    nc.gpsimd.tensor_tensor(keep[:, 1:2], gate[:, 0:1], col[:, 2:3], ALU.mult).then_inc(keep_made, 1)
                gb = summed_block(k - 1)
                if gb is not None and BLOCKS[gb][0] == 1:
                    _, b, h = BLOCKS[gb]
                    n = out_count(gb, 0)
                    pool.wait_ge(r_inv_ready, blocks(gb, it))
                    if n > 1 or not isinstance(it, int):
                        last = ORDER["r", b, 0] if h else ORDER["r", b - 1, 1] if b else ORDER["r", b, 1] - GROUPS_PER_PERIOD
                        pool.wait_ge(misc_ready, last + 1 + GROUPS_PER_PERIOD * it)
                    round_to(r_hi[:, :], r_inv[:, slot(gb), :]).then_inc(r_split, 1)
                    pool.wait_ge(r_split, 2 * n - 1 + 4 * it)
                    nc.gpsimd.tensor_tensor(r_lo[:, :], r_inv[:, slot(gb), :], f(r_hi[:, :]), ALU.subtract).then_inc(r_split, 1)
                    pool.wait_ge(r_split, 2 * n + 4 * it)
                    eye = ident[:, :].unsqueeze(1).broadcast_to([P, TPB, P])
                    for diag, r in ((diag_hi, f(r_hi[:, :])), (diag_lo, r_lo[:, :])):
                        nc.gpsimd.tensor_tensor(diag[:, :].rearrange("p (n q) -> p n q", n=TPB), eye,
                                                r.unsqueeze(2).broadcast_to([P, TPB, P]), ALU.mult).then_inc(diag_ready, 1)
                for group in SCHEDULE[k][0] + SCHEDULE[k][1]:
                    small(group, it)
                gb = drained_block(k)
                if gb is not None and BLOCKS[gb][0] == 1:
                    _, b, h = BLOCKS[gb]
                    pool.wait_ge(accum_drained, blocks(gb, it))
                    pool.wait_ge(misc_drained, groups(("f", b, h), it))
                    nc.gpsimd.tensor_tensor(o_sb[:, cols(h)], o_sb[:, cols(h)], f_part[:, cols(h)],
                                            ALU.add).then_inc(out_ready, 1)
            steps(pool, emit)


def kernel(x, L0_conv_theta_w, L0_conv_theta_b, L0_conv_phi_w, L0_conv_phi_b, L0_conv_g_w, L0_conv_g_b,
           L0_conv_wz_w, L0_conv_wz_b, L0_conv_w, L1_conv_Wq, L1_conv_bq, L1_conv_Wk, L1_conv_bk, L1_conv_Wv,
           L1_conv_bv, L1_conv_gamma, L1_conv_Wf, L1_conv_bf):
    import numpy as np
    import concourse.bacc as bacc
    from concourse.bass_utils import run_bass_kernel_spmd

    def a(v):
        return np.asarray(v)

    f1, f2 = a(L1_conv_Wf)[:, :C], a(L1_conv_Wf)[:, C:]
    qk = np.zeros((P, 2), np.float32)
    for n in range(3):
        qk[ROW * n:ROW * n + CK, 0] = a(L1_conv_bq)
        qk[ROW * n:ROW * n + CK, 1] = a(L1_conv_bk)
    arrays = {
        "x": np.ascontiguousarray(a(x).reshape(B, C, N)),
        "weights_t": np.ascontiguousarray(np.concatenate(
            [a(L0_conv_theta_w).T, a(L0_conv_phi_w).T, a(L0_conv_g_w).T, a(L0_conv_wz_w).T, f2.T, f1.T,
             a(L1_conv_Wv), a(L1_conv_Wq).T, a(L1_conv_Wk).T], axis=1)),
        "columns": np.ascontiguousarray(np.stack(
            [a(L0_conv_theta_b), a(L0_conv_phi_b), a(L0_conv_wz_b), a(L1_conv_bv), a(L1_conv_bf)], axis=1)),
        "qk_bias": qk,
        "g_bias": np.ascontiguousarray(a(L0_conv_g_b)),
        "gates": np.stack([a(L0_conv_w), a(L1_conv_gamma)]),
    }
    nc = bacc.Bacc("TRN2", target_bir_lowering=False, num_devices=1)
    args = [nc.dram_tensor(f"{name}_dram", v.shape, mybir.dt.from_np(v.dtype), kind="ExternalInput").ap()
            for name, v in arrays.items()]
    out = nc.dram_tensor("out_dram", (B, C, N), mybir.dt.float32, kind="ExternalOutput").ap()
    build(nc, *args, out)
    r = run_bass_kernel_spmd(nc, [{f"{name}_dram": v for name, v in arrays.items()}], core_ids=[0])
    return r.results[0]["out_dram"].reshape(B, C, 32, 32)
```

```python
from contextlib import ExitStack

import concourse.bass as bass
from concourse import mybir

B, C, N, CK = 8, 128, 1024, 16
P = 128
HALF = N // 2
TPB = HALF // P
KT = N // P
CPB = 4
ROW = 32
KROWS = 3 * ROW

BLOCKS = []
for _i in range(B + 2):
    if _i < B:
        BLOCKS.append((0, _i, 0))
    if 0 <= _i - 2:
        BLOCKS.append((1, _i - 2, 1))
    if _i < B:
        BLOCKS.append((0, _i, 1))
    if 0 <= _i - 1 < B:
        BLOCKS.append((1, _i - 1, 0))
UNITS = TPB * len(BLOCKS)
PERIOD = 16
LOOP_FROM, LOOP_TRIPS = 20, 5
LOOP_TO = LOOP_FROM + PERIOD * LOOP_TRIPS
LAST_STEP = UNITS + 4


def block_index(layer, b, h):
    return BLOCKS.index((layer, b, h))


def _schedule():
    at = {k: ([], []) for k in range(LAST_STEP)}

    def put(k, when, *groups):
        at[k][when].extend(groups)

    put(0, 0, ("g", 0, 0))
    put(1, 0, ("g", 0, 1))
    put(2, 0, ("setup", 0, 0))
    put(4, 1, ("theta", 1, 0))
    put(5, 1, ("theta", 1, 1))
    put(6, 1, ("phi", 1, 0))
    put(7, 0, ("phi", 1, 1))
    put(8, 0, ("y", 0, 0))
    put(9, 0, ("z", 0, 0))
    put(12, 0, ("g", 1, 0))
    put(12, 1, ("y", 0, 1))
    put(13, 0, ("g", 1, 1))
    put(13, 1, ("z", 0, 1))
    put(14, 0, ("k", 0, 0))
    put(14, 1, ("k", 0, 1))
    put(15, 0, ("q", 0, 0))
    put(15, 1, ("f", 0, 0))
    put(16, 0, ("q", 0, 1))
    put(16, 1, ("theta", 2, 0))
    put(17, 0, ("theta", 2, 1))
    put(17, 1, ("phi", 2, 0))
    put(18, 0, ("f", 0, 1))
    put(18, 1, ("phi", 2, 1))
    put(19, 0, ("v", 0, 0))
    put(19, 1, ("v", 0, 1))
    for i in range(2, B):
        k = LOOP_FROM + PERIOD * (i - 2)
        put(k, 0, ("y", i - 1, 0))
        put(k + 1, 1, ("z", i - 1, 0))
        put(k + 2, 0, ("g", i, 0))
        put(k + 2, 1, ("y", i - 1, 1))
        put(k + 3, 1, ("g", i, 1))
        put(k + 4, 1, ("z", i - 1, 1))
        put(k + 5, 0, ("r", i - 2, 0))
        put(k + 6, 0, ("q", i - 1, 0))
        put(k + 7, 0, ("f", i - 1, 0))
        put(k + 7, 1, ("k", i - 1, 0))
        put(k + 8, 1, ("k", i - 1, 1))
        put(k + 9, 1, ("q", i - 1, 1))
        put(k + 10, 1, ("r", i - 2, 1))
        if i + 1 < B:
            put(k + 11, 1, ("theta", i + 1, 0))
            put(k + 12, 1, ("theta", i + 1, 1))
            put(k + 13, 0, ("phi", i + 1, 0))
            put(k + 13, 1, ("phi", i + 1, 1))
        put(k + 14, 1, ("v", i - 1, 0))
        put(k + 15, 0, ("f", i - 1, 1))
        put(k + 15, 1, ("v", i - 1, 1))
    t = LOOP_FROM + PERIOD * (B - 2)
    put(t - 1, 1, ("y", B - 1, 0))
    put(t, 0, ("z", B - 1, 0))
    put(t, 1, ("y", B - 1, 1))
    put(t + 1, 0, ("k", B - 1, 0))
    put(t + 1, 1, ("z", B - 1, 1))
    put(t + 2, 0, ("q", B - 1, 0))
    put(t + 2, 1, ("k", B - 1, 1))
    put(t + 3, 0, ("r", B - 2, 0))
    put(t + 3, 1, ("q", B - 1, 1))
    put(t + 4, 0, ("v", B - 1, 0))
    put(t + 4, 1, ("v", B - 1, 1))
    put(t + 5, 1, ("f", B - 1, 0))
    put(t + 6, 1, ("r", B - 2, 1))
    put(t + 9, 0, ("f", B - 1, 1))
    put(t + 11, 0, ("r", B - 1, 0))
    put(t + 14, 1, ("r", B - 1, 1))
    return at


SCHEDULE = _schedule()
ORDER = {}
for _k in range(LAST_STEP):
    for _g in SCHEDULE[_k][0] + SCHEDULE[_k][1]:
        ORDER[_g] = len(ORDER)
LOOP_GROUPS = sum(len(SCHEDULE[k][0] + SCHEDULE[k][1]) for k in range(LOOP_FROM))
GROUPS_PER_PERIOD = sum(len(SCHEDULE[k][0] + SCHEDULE[k][1]) for k in range(LOOP_FROM, LOOP_FROM + PERIOD))

HURRIED = {0: (6, 6, 7, 7), 1: (10, 10, 11, 11), 27: (114, 114, 115, 115), 28: (118, 118, 119, 119),
           29: (122, 122, 123, 123), 30: (126, 126, 127, 127), 31: (130, 130, 130, 130)}
VALUE_STEPS = [HURRIED.get(gb, tuple(TPB * gb + 6 + c for c in range(CPB))) for gb in range(len(BLOCKS))]

SPLIT_X = {2: 1, 15: 2, **{LOOP_FROM + PERIOD * (i - 2) + 9: i + 1 for i in range(2, B - 1)}}
KEEP_X = {0: 0, 5: 1, **{LOOP_FROM + PERIOD * (i - 2) + 6: i for i in range(2, B)}}
LOAD_X = {0: 1, 6: 2, **{LOOP_FROM + PERIOD * (i - 2) + 7: i + 1 for i in range(2, B - 1)}}

W_THETA, W_PHI, W_G, W_Z, W_F2, W_F1, W_V, W_Q = range(0, 8 * P, P)
W_K = W_Q + CK
W_COLS = 7 * P + 2 * CK
SPLIT_COLS = 5 * P


def build(nc, x, weights_t, columns, qk_bias, g_bias, gates, out):
    f32, f32r = mybir.dt.float32, mybir.dt.float32r
    ALU, ACT, AX = mybir.AluOpType, mybir.ActivationFunctionType, mybir.AxisListType

    with ExitStack() as ctx:
        def sb(name, shape, dt=f32):
            return ctx.enter_context(nc.sbuf_tensor(name, shape, dt))

        def sem(name):
            return ctx.enter_context(nc.semaphore(name))

        w_all = sb("w_all", [P, W_COLS])
        w_hi = sb("w_hi", [P, SPLIT_COLS], f32r)
        w_lo = sb("w_lo", [P, SPLIT_COLS], f32r)
        wqk = sb("wqk", [P, 2, 3, ROW])
        wqk_hi = sb("wqk_hi", [P, 2, KROWS], f32r)
        wqk_lo = sb("wqk_lo", [P, 2, KROWS], f32r)
        wv = sb("wv", [P, P])
        wv_hi = sb("wv_hi", [P, P], f32r)
        wv_lo = sb("wv_lo", [P, P], f32r)
        v_bias = sb("v_bias", [P, P])
        g_bias_rows = sb("g_bias_rows", [P, P])
        bv_cols = sb("bv_cols", [P, P])
        col = sb("col", [P, 5])
        qk_b = sb("qk_b", [P, 2])
        gate = sb("gate", [P, 2])
        keep = sb("keep", [P, 2])
        ident = sb("ident", [P, P])
        ones = sb("ones", [P, P])
        ones_r = sb("ones_r", [P, P], f32r)
        zero = sb("zero", [P, 1])
        warm = sb("warm", [P, 1])

        x_raw = sb("x_raw", [P, N])
        x_hi = sb("x_hi", [P, N], f32r)
        x_lo = sb("x_lo", [P, N], f32r)
        x_keep_0 = sb("x_keep_0", [P, N])
        x_keep = sb("x_keep", [P, N])
        theta_hi = sb("theta_hi", [P, N], f32r)
        theta_lo = sb("theta_lo", [P, N], f32r)
        phi_hi = sb("phi_hi", [P, N], f32r)
        phi_lo = sb("phi_lo", [P, N], f32r)
        proj_full = sb("proj_full", [P, 2, HALF])
        g_full = sb("g_full", [P, HALF])
        g_hi = sb("g_hi", [P, N], f32r)
        g_lo = sb("g_lo", [P, N], f32r)
        v_full = sb("v_full", [P, HALF])
        v_hi = sb("v_hi", [P, N], f32r)
        v_lo = sb("v_lo", [P, N], f32r)
        q_op = sb("q_op", [KROWS, N], f32r)
        k_op = sb("k_op", [KROWS, N], f32r)
        probs = sb("probs", [P, 2, N])
        pt_hi = sb("pt_hi", [P, 2, KT, HALF], f32r)
        pt_lo = sb("pt_lo", [P, 2, KT, HALF], f32r)
        neg_max = sb("neg_max", [P, 4])
        row_sum = sb("row_sum", [P, 4, TPB])
        r_inv = sb("r_inv", [P, 4, TPB])
        r_hi = sb("r_hi", [P, TPB], f32r)
        r_lo = sb("r_lo", [P, TPB])
        diag_hi = sb("diag_hi", [P, HALF], f32r)
        diag_lo = sb("diag_lo", [P, HALF], f32r)
        r_rows = sb("r_rows", [P, HALF])
        ut = sb("ut", [P, 2, HALF])
        y_full = sb("y_full", [P, HALF])
        y_hi = sb("y_hi", [P, HALF], f32r)
        y_lo = sb("y_lo", [P, HALF], f32r)
        z_full = sb("z_full", [P, HALF])
        z_hi = sb("z_hi", [P, N], f32r)
        z_lo = sb("z_lo", [P, N], f32r)
        f_part = sb("f_part", [P, N])
        o_sb = sb("o_sb", [P, N])

        def theta_of(b):
            return (v_hi, v_lo) if b == 0 else (theta_hi, theta_lo)

        def phi_of(b):
            return (z_hi, z_lo) if b == 0 else (phi_hi, phi_lo)

        def q_of(b):
            return theta_hi if b == B - 1 else q_op

        def k_of(b):
            return phi_hi if b == B - 1 else k_op

        def v_of(b):
            return (g_hi, g_lo) if b == B - 1 else (v_hi, v_lo)

        scores = ctx.enter_context(nc.psum_tensor("scores", [P, 2, N], f32))
        trans = ctx.enter_context(nc.psum_tensor("trans", [P, N], f32))
        accum = ctx.enter_context(nc.psum_tensor("accum", [P, HALF], f32))
        misc = ctx.enter_context(nc.psum_tensor("misc", [P, HALF], f32))

        weights_loaded = sem("weights_loaded")
        rest_loaded = sem("rest_loaded")
        small_loaded = sem("small_loaded")
        x_loaded = sem("x_loaded")
        ident_ready = sem("ident_ready")
        consts_ready = sem("consts_ready")
        zero_ready = sem("zero_ready")
        w_split = sem("w_split")
        rest_split = sem("rest_split")
        wqk_made = sem("wqk_made")
        wqk_split = sem("wqk_split")
        setup_done = sem("setup_done")
        wv_split = sem("wv_split")
        x_split = sem("x_split")
        x_kept = sem("x_kept")
        scores_ready = sem("scores_ready")
        max_ready = sem("max_ready")
        probs_ready = sem("probs_ready")
        trans_ready = sem("trans_ready")
        pt_hi_ready = sem("pt_hi_ready")
        pt_lo_ready = sem("pt_lo_ready")
        pv_done = sem("pv_done")
        accum_drained = sem("accum_drained")
        r_inv_ready = sem("r_inv_ready")
        misc_ready = sem("misc_ready")
        misc_drained = sem("misc_drained")
        op_hi_ready = sem("op_hi_ready")
        proj_split = sem("proj_split")
        first_ready = sem("first_ready")
        first_hi = sem("first_hi")
        x_first = [sem("x_first_0"), sem("x_first_1")]
        x_first_hi = sem("x_first_hi")
        r_split = sem("r_split")
        keep_made = sem("keep_made")
        diag_ready = sem("diag_ready")
        g_split = sem("g_split")
        v_split = sem("v_split")
        y_split = sem("y_split")
        z_split = sem("z_split")
        out_ready = sem("out_ready")
        stored = [sem("stored_0"), sem("stored_1")]

        def units(k, it):
            return k + 1 + PERIOD * it

        def banks(k, bank, it):
            return 2 * k + bank + 1 + 2 * PERIOD * it

        def blocks(gb, it):
            return gb + 1 + (PERIOD // TPB) * it

        def chunks(gb, c, it):
            return CPB * gb + c + 1 + PERIOD * it

        def groups(group, it):
            n = ORDER[group]
            if not isinstance(it, int) and n < LOOP_GROUPS:
                kind, b, h = group
                n = max(n, ORDER[kind, b + 1, h] - GROUPS_PER_PERIOD)
            return n + 1 + GROUPS_PER_PERIOD * it

        def halves(b, h, it, each=1):
            return each * (2 * b + h + 1) + 2 * each * it

        def ops(kind, b, h, it):
            before = [g for g in ORDER if g[0] in ("q", "k") and ORDER[g] <= ORDER[(kind, b, h)]]
            return len(before) + 4 * it

        def projection(kind, b, h, it):
            return 8 * b + 4 * (kind == "phi") + 2 * h + 2 + 8 * it

        def out_count(gb, it):
            return sum(1 for n in range(gb + 1) if BLOCKS[n][0] == 1) + 2 * it

        def cols(h):
            return slice(h * HALF, (h + 1) * HALF)

        def f(ap):
            return ap.bitcast(f32)

        def steps(engine, emit):
            for k in range(LOOP_FROM):
                emit(k, 0)
            with engine.Fori(0, LOOP_TRIPS) as it:
                for k in range(LOOP_FROM, LOOP_FROM + PERIOD):
                    emit(k, it)
            for k in range(LOOP_TO, LAST_STEP):
                emit(k, 0)

        def slot(gb):
            layer, _, h = BLOCKS[gb]
            return 2 * layer + h

        def last_of_slot(gb):
            layer, b, h = BLOCKS[gb]
            return block_index(layer, b - 1, h) if b else gb - PERIOD // TPB

        def drained_block(k):
            ended = [gb for gb in range(len(BLOCKS)) if VALUE_STEPS[gb][-1] == k - 1]
            return ended[0] if ended else None

        def summed_block(k):
            gb, off = divmod(k - 5, TPB)
            return gb if off == 0 and 0 <= gb < len(BLOCKS) else None

        block = ctx.enter_context(nc.Block())

        @block.sync
        def _(sp):
            for h in range(2):
                sp.dma_start(x_raw[:, cols(h)], x[0, :, cols(h)]).then_inc(x_first[h], 16)
            sp.dma_start(col[:, :], columns).then_inc(small_loaded, 16)
            sp.dma_start(qk_b[:, :], qk_bias).then_inc(small_loaded, 16)
            sp.dma_start(gate[:, :], gates.partition_broadcast(P)).then_inc(small_loaded, 16)
            sp.dma_start(g_bias_rows[:, :], g_bias.partition_broadcast(P)).then_inc(small_loaded, 16)

            def emit(k, it):
                if k in LOAD_X:
                    b = LOAD_X[k]
                    sp.wait_ge(x_kept, b + it)
                    sp.dma_start(x_raw[:, :], x[b + it]).then_inc(x_loaded, 16)
                gb = drained_block(k)
                if gb is not None and BLOCKS[gb][0] == 1:
                    _, b, h = BLOCKS[gb]
                    sp.wait_ge(out_ready, out_count(gb, it))
                    sp.dma_start(out[b + it, :, cols(h)], o_sb[:, cols(h)]).then_inc(stored[h], 16)
            steps(sp, emit)
            for h in range(2):
                sp.wait_ge(stored[h], 16 * B)

        @block.tensor
        def _(pe):
            def three(dst, hi_l, lo_l, hi_r, lo_r):
                nc.tensor.matmul(dst, hi_l, hi_r, start=True, stop=False)
                nc.tensor.matmul(dst, hi_l, lo_r, start=False, stop=False)
                return nc.tensor.matmul(dst, lo_l, hi_r, start=False, stop=True)

            def unit_scores(k, it):
                layer, b, h = BLOCKS[k // TPB]
                t = k % TPB
                if k >= 2:
                    pe.wait_ge(probs_ready, units(k - 2, it))
                if t == 0 and layer == 0:
                    pe.wait_ge(proj_split, projection("phi", b, 1, it))
                if t == 0 and layer == 1:
                    pe.wait_ge(misc_drained, groups(("q", b, 0) if h == 0 else ("q", b, 1), it))
                for half in range(2):
                    dst = scores[:, k % 2, cols(half)]
                    if layer == 0:
                        queries = slice(TPB * h + t, N, KT)
                        (t_hi, t_lo), (p_hi, p_lo) = theta_of(b), phi_of(b)
                        last = three(dst, t_hi[:, queries], t_lo[:, queries], p_hi[:, cols(half)], p_lo[:, cols(half)])
                    else:
                        q0 = h * HALF + t * P
                        last = nc.tensor.matmul(dst, q_of(b)[0:KROWS, q0:q0 + P], k_of(b)[0:KROWS, cols(half)],
                                                start=True, stop=True)
                last.then_inc(scores_ready, 1)

            def unit_transposes(k, it):
                pe.wait_ge(probs_ready, units(k, it))
                for bank in range(2):
                    if k >= 1:
                        pe.wait_ge(pt_lo_ready, banks(k - 1, bank, it))
                    for n in range(4 * bank, 4 * bank + 4):
                        last = nc.tensor.transpose(trans[:, n * P:(n + 1) * P], probs[:, k % 2, n * P:(n + 1) * P],
                                                   ident[:, :])
                    last.then_inc(trans_ready, 1)

            def value_chunk(gb, c, it):
                layer, b, h = BLOCKS[gb]
                hi, lo = (g_hi, g_lo) if layer == 0 else v_of(b)
                if c == 0:
                    pe.wait_ge(pt_lo_ready, banks(TPB * gb + TPB - 1, 1, it))
                    pe.wait_ge(g_split if layer == 0 else v_split, halves(b, 1, it, 2))
                    if gb:
                        pe.wait_ge(accum_drained, blocks(gb - 1, it))
                for n in range(2 * c, 2 * c + 2):
                    tile = slice(n * P, (n + 1) * P)
                    p_hi, p_lo = pt_hi[:, gb % 2, n, :], pt_lo[:, gb % 2, n, :]
                    nc.tensor.matmul(accum[:, :], hi[:, tile], p_hi, start=(n == 0), stop=False)
                    nc.tensor.matmul(accum[:, :], hi[:, tile], p_lo, start=False, stop=False)
                    last = nc.tensor.matmul(accum[:, :], lo[:, tile], p_hi, start=False, stop=(n == KT - 1))
                last.then_inc(pv_done, 1)

            def small(group, it):
                kind, b, h = group
                if ORDER[group]:
                    pe.wait_ge(misc_drained, ORDER[group] + GROUPS_PER_PERIOD * it)
                if kind in ("theta", "phi"):
                    w0 = W_THETA if kind == "theta" else W_PHI
                    pe.wait_ge(x_split, 2 * (b + 1) + 2 * it)
                    last = three(misc[:, :], w_hi[:, w0:w0 + P], w_lo[:, w0:w0 + P], x_hi[:, cols(h)], x_lo[:, cols(h)])
                elif kind in ("g", "v"):
                    if kind == "g":
                        pe.wait_ge(x_split, 2 * (b + 1) + 2 * it)
                        m_hi, m_lo, r_h, r_l = x_hi, x_lo, w_hi[:, W_G:W_G + P], w_lo[:, W_G:W_G + P]
                    else:
                        pe.wait_ge(z_split, halves(b, h, it, 2))
                        m_hi, m_lo, r_h, r_l = z_hi, z_lo, wv_hi[:, :], wv_lo[:, :]
                    for n in range(4):
                        tile = slice(h * HALF + n * P, h * HALF + (n + 1) * P)
                        last = three(misc[:, n * P:(n + 1) * P], m_hi[:, tile], m_lo[:, tile], r_h, r_l)
                elif kind == "y":
                    pe.wait_ge(accum_drained, blocks(block_index(0, b, h), it))
                    for n in range(4):
                        last = nc.tensor.transpose(misc[:, n * P:(n + 1) * P], ut[:, h, n * P:(n + 1) * P], ident[:, :])
                elif kind == "z":
                    pe.wait_ge(y_split, halves(b, h, it, 2))
                    last = three(misc[:, :], w_hi[:, W_Z:W_Z + P], w_lo[:, W_Z:W_Z + P], y_hi[:, :], y_lo[:, :])
                elif kind in ("q", "k"):
                    i = 0 if kind == "q" else 1
                    pe.wait_ge(z_split, halves(b, h, it, 2))
                    last = three(misc[0:KROWS, :], wqk_hi[:, i, :], wqk_lo[:, i, :], z_hi[:, cols(h)], z_lo[:, cols(h)])
                elif kind == "f":
                    last = three(misc[:, :], w_hi[:, W_F2:W_F2 + P], w_lo[:, W_F2:W_F2 + P],
                                 z_hi[:, cols(h)], z_lo[:, cols(h)])
                elif kind == "r":
                    pe.wait_ge(diag_ready, 2 * out_count(block_index(1, b, h), it))
                    nc.tensor.matmul(misc[:, :], ones_r[:, :], diag_hi[:, :], start=True, stop=False)
                    last = nc.tensor.matmul(misc[:, :], ones_r[:, :], diag_lo[:, :], start=False, stop=True)
                else:
                    pe.wait_ge(consts_ready, 4)
                    nc.tensor.matmul(misc[:, 0:P], w_all[:, W_V:W_V + P], w_all[:, W_F1:W_F1 + P], start=True, stop=True)
                    last = nc.tensor.matmul(misc[:, P:2 * P], bv_cols[:, :], w_all[:, W_F1:W_F1 + P],
                                            start=True, stop=True)
                last.then_inc(misc_ready, 1)

            pe.wait_ge(w_split, 2)
            for h in range(2):
                pe.wait_ge(x_split, h + 1)
                for i, w0 in enumerate((W_THETA, W_PHI)):
                    three(scores[:, i, cols(h)], w_hi[:, w0:w0 + P], w_lo[:, w0:w0 + P],
                          x_hi[:, cols(h)], x_lo[:, cols(h)]).then_inc(first_ready, 1)

            def emit(k, it):
                if 0 <= k < UNITS:
                    unit_scores(k, it)
                if k == 0:
                    pe.wait_ge(rest_split, 2)
                    pe.wait_ge(ident_ready, 2)
                if k == 14:
                    pe.wait_ge(wqk_split, 2)
                if k == 19:
                    pe.wait_ge(wv_split, 2)
                before, after = SCHEDULE[k]
                for group in before:
                    small(group, it)
                for gb in range(len(BLOCKS)):
                    for c in range(CPB):
                        if VALUE_STEPS[gb][c] == k:
                            value_chunk(gb, c, it)
                for group in after:
                    small(group, it)
                if 0 <= k - 1 < UNITS:
                    unit_transposes(k - 1, it)
            steps(pe, emit)

        @block.scalar
        def _(act):
            act.dma_start(w_all[:, 0:2 * P], weights_t[:, 0:2 * P]).then_inc(weights_loaded, 16)
            act.dma_start(w_all[:, 2 * P:W_COLS], weights_t[:, 2 * P:W_COLS]).then_inc(rest_loaded, 16)
            act.wait_ge(consts_ready, 1)
            nc.scalar.activation(warm[:, :], ones[:, 0:1], ACT.Exp)
            for h in range(2):
                act.wait_ge(x_first[h], 16)
                nc.scalar.activation(x_hi[:, cols(h)], x_raw[:, cols(h)], ACT.Copy).then_inc(x_first_hi, 1)
            act.wait_ge(small_loaded, 64)
            for n, (h, i) in enumerate(((0, 0), (0, 1), (1, 0), (1, 1))):
                act.wait_ge(first_ready, n + 1)
                hi, _ = theta_of(0) if i == 0 else phi_of(0)
                nc.scalar.activation(hi[:, cols(h)], scores[:, i, cols(h)], ACT.Identity,
                                     bias=col[:, i:i + 1]).then_inc(first_hi, 1)

            def unit_exp(k, it):
                gb, t = divmod(k, TPB)
                act.wait_ge(max_ready, units(k, it))
                if k >= 2:
                    act.wait_ge(trans_ready, banks(k - 2, 1, it))
                if t == 0 and gb >= 5:
                    act.wait_ge(r_inv_ready, blocks(last_of_slot(gb), it))
                nc.scalar.activation(probs[:, k % 2, :], scores[:, k % 2, :], ACT.Exp, bias=neg_max[:, k % 4:k % 4 + 1],
                                     accum_out=row_sum[:, slot(gb), t:t + 1]).then_inc(probs_ready, 1)

            def unit_hi(k, it):
                gb, t = divmod(k, TPB)
                for bank in range(2):
                    act.wait_ge(trans_ready, banks(k, bank, it))
                    if t == 0 and bank == 0 and gb >= 2:
                        act.wait_ge(pv_done, chunks(gb - 2, CPB - 1, it))
                    nc.scalar.activation(pt_hi[:, gb % 2, 4 * bank:4 * bank + 4, t * P:(t + 1) * P],
                                         trans[:, cols(bank)].rearrange("p (n q) -> p n q", n=4),
                                         ACT.Copy).then_inc(pt_hi_ready, 1)

            def small(group, it):
                kind, b, h = group
                if kind not in ("theta", "phi", "q", "k", "f", "r"):
                    return
                act.wait_ge(misc_ready, groups(group, it))
                if kind in ("theta", "phi"):
                    c = 0 if kind == "theta" else 1
                    if projection(kind, b, h, 0) > 4:
                        act.wait_ge(proj_split, projection(kind, b, h, it) - 4)
                    nc.scalar.activation(proj_full[:, h, :], misc[:, :], ACT.Identity,
                                         bias=col[:, c:c + 1]).then_inc(misc_drained, 1)
                elif kind in ("q", "k"):
                    dst, c = (q_of(b), 0) if kind == "q" else (k_of(b), 1)
                    nc.scalar.activation(dst[0:KROWS, cols(h)], misc[0:KROWS, :], ACT.Identity,
                                         bias=qk_b[0:KROWS, c:c + 1]).then_inc(op_hi_ready, 1)
                elif kind == "f":
                    if b > 0:
                        act.wait_ge(out_ready, out_count(block_index(1, b - 1, h), it))
                    nc.scalar.activation(f_part[:, cols(h)], misc[:, :], ACT.Identity,
                                         bias=col[:, 4:5]).then_inc(misc_drained, 1)
                else:
                    nc.scalar.activation(r_rows[:, :], misc[:, :], ACT.Copy).then_inc(misc_drained, 1)

            def keep_x(b, it):
                act.wait_ge(x_split, 2 * b + 2 + 2 * it)
                if b >= 2:
                    act.wait_ge(misc_drained, groups(("z", b - 1, 1), it))
                dst = x_keep_0 if b == 0 else x_keep
                nc.scalar.activation(dst[:, :], x_raw[:, :], ACT.Identity, scale=keep[:, 0:1],
                                     bias=keep[:, 1:2]).then_inc(x_kept, 1)

            def emit(k, it):
                gb = drained_block(k)
                if gb is not None and BLOCKS[gb][0] == 0:
                    _, b, h = BLOCKS[gb]
                    act.wait_ge(pv_done, chunks(gb, CPB - 1, it))
                    if b > 0:
                        act.wait_ge(misc_ready, groups(("y", b - 1, h), it))
                    nc.scalar.activation(ut[:, h, :], accum[:, :], ACT.Copy).then_inc(accum_drained, 1)
                if 0 <= k - 2 < UNITS:
                    unit_hi(k - 2, it)
                if 0 <= k - 1 < UNITS:
                    unit_exp(k - 1, it)
                for group in SCHEDULE[k][0] + SCHEDULE[k][1]:
                    small(group, it)
                if k in KEEP_X:
                    if k == 0:
                        act.wait_ge(keep_made, 2)
                    keep_x(KEEP_X[k], it)
            steps(act, emit)

        @block.vector
        def _(dve):
            nc.vector.memset(ones[:, :], 1.0).then_inc(consts_ready, 1)
            nc.vector.memset(ones_r[:, :].bitcast(f32), 1.0).then_inc(consts_ready, 1)
            nc.vector.memset(wqk[:, :, :, :], 0.0).then_inc(wqk_made, 1)
            dve.wait_ge(weights_loaded, 16)
            nc.vector.tensor_copy(w_hi[:, 0:2 * P], w_all[:, 0:2 * P]).then_inc(w_split, 1)
            dve.wait_ge(w_split, 1)
            nc.vector.tensor_tensor(w_lo[:, 0:2 * P], w_all[:, 0:2 * P], f(w_hi[:, 0:2 * P]),
                                    ALU.subtract).then_inc(w_split, 1)
            for h in range(2):
                dve.wait_ge(x_first_hi, h + 1)
                nc.vector.tensor_tensor(x_lo[:, cols(h)], x_raw[:, cols(h)], f(x_hi[:, cols(h)]),
                                        ALU.subtract).then_inc(x_split, 1)
            dve.wait_ge(small_loaded, 64)
            for n, (h, i) in enumerate(((0, 0), (0, 1), (1, 0), (1, 1))):
                dve.wait_ge(first_hi, n + 1)
                hi, lo = theta_of(0) if i == 0 else phi_of(0)
                nc.vector.scalar_tensor_tensor(lo[:, cols(h)], scores[:, i, cols(h)], col[:, i:i + 1], f(hi[:, cols(h)]),
                                               ALU.add, ALU.subtract).then_inc(proj_split, 2)

            def late_setup():
                dve.wait_ge(rest_loaded, 16)
                dve.wait_ge(consts_ready, 2)
                nc.vector.tensor_scalar(bv_cols[:, :], ones[:, :], col[:, 3:4], None, ALU.mult).then_inc(consts_ready, 1)
                nc.vector.tensor_scalar(qk_b[:, 0:1], qk_b[:, 0:1], CK ** -0.5, None, ALU.mult).then_inc(consts_ready, 1)
                dve.wait_ge(wqk_made, 1)
                for i, (w0, scale) in enumerate(((W_Q, CK ** -0.5), (W_K, 1.0))):
                    for n in range(3):
                        nc.vector.tensor_scalar(wqk[:, i, n, 0:CK], w_all[:, w0:w0 + CK], scale, None,
                                                ALU.mult).then_inc(wqk_made, 1)
                dve.wait_ge(wqk_made, 7)
                flat = wqk[:, :, :, :].rearrange("p i n c -> p i (n c)")
                nc.vector.tensor_copy(wqk_hi[:, :, :], flat).then_inc(wqk_split, 1)
                dve.wait_ge(wqk_split, 1)
                nc.vector.tensor_tensor(wqk_lo[:, :, :], flat, f(wqk_hi[:, :, :]), ALU.subtract).then_inc(wqk_split, 1)

            def unit_max(k, it):
                dve.wait_ge(scores_ready, units(k, it))
                if k >= 4:
                    dve.wait_ge(probs_ready, units(k - 4, it))
                nc.vector.tensor_reduce(neg_max[:, k % 4:k % 4 + 1], scores[:, k % 2, :], AX.X, ALU.max,
                                        negate=True).then_inc(max_ready, 1)

            def unit_lo(k, it):
                gb, t = divmod(k, TPB)
                for bank in range(2):
                    dve.wait_ge(pt_hi_ready, banks(k, bank, it))
                    if t == 0 and bank == 0 and gb >= 2:
                        dve.wait_ge(pv_done, chunks(gb - 2, CPB - 1, it))
                    at = (slice(None), gb % 2, slice(4 * bank, 4 * bank + 4), slice(t * P, (t + 1) * P))
                    nc.vector.tensor_tensor(pt_lo[at], trans[:, cols(bank)].rearrange("p (n q) -> p n q", n=4),
                                            f(pt_hi[at]), ALU.subtract).then_inc(pt_lo_ready, 1)

            def small(group, it):
                kind, b, h = group
                if kind in ("theta", "phi", "f", "r"):
                    return
                if kind in ("q", "k"):
                    dve.wait_ge(op_hi_ready, ops(kind, b, h, it))
                    dst, c, r0 = (q_of(b), 0, ROW) if kind == "q" else (k_of(b), 1, 2 * ROW)
                    rows = slice(r0, r0 + ROW)
                    nc.vector.scalar_tensor_tensor(dst[rows, cols(h)], misc[rows, :], qk_b[rows, c:c + 1],
                                                   f(dst[rows, cols(h)]), ALU.add,
                                                   ALU.subtract).then_inc(misc_drained, 1)
                    return
                dve.wait_ge(misc_ready, groups(group, it))
                four = misc[:, :].rearrange("p (n c) -> p n c", n=4)
                if kind in ("g", "v"):
                    full, bias, split = (g_full, g_bias_rows, g_split) if kind == "g" else (v_full, v_bias, v_split)
                    if 2 * b + h:
                        dve.wait_ge(split, halves(b, h, it, 2) - 2)
                    if kind == "v" and (b, h) == (0, 0):
                        dve.wait_ge(setup_done, 1)
                    nc.vector.tensor_tensor(full[:, :].rearrange("p (n c) -> p n c", n=4), four,
                                            bias[:, :].unsqueeze(1).broadcast_to([P, 4, P]),
                                            ALU.add).then_inc(misc_drained, 1)
                elif kind == "y":
                    if 2 * b + h:
                        dve.wait_ge(y_split, halves(b, h, it, 2) - 2)
                    gb = block_index(0, b, h)
                    dve.wait_ge(r_inv_ready, blocks(gb, it))
                    nc.vector.tensor_tensor(y_full[:, :].rearrange("p (n c) -> p n c", n=4), four,
                                            r_inv[:, slot(gb), :].unsqueeze(2).broadcast_to([P, 4, P]),
                                            ALU.mult).then_inc(misc_drained, 1)
                elif kind == "z":
                    if 2 * b + h:
                        dve.wait_ge(z_split, halves(b, h, it, 2) - 2)
                    dve.wait_ge(x_kept, b + 1 + it)
                    keep_of = x_keep_0 if b == 0 else x_keep
                    nc.vector.scalar_tensor_tensor(z_full[:, :], misc[:, :], gate[:, 0:1], keep_of[:, cols(h)],
                                                   ALU.mult, ALU.add).then_inc(misc_drained, 1)
                else:
                    nc.vector.tensor_scalar(v_bias[:, :], misc[:, P:2 * P], gate[:, 1:2], None,
                                            ALU.mult).then_inc(setup_done, 1)
                    nc.vector.tensor_scalar(wv[:, :], misc[:, 0:P], gate[:, 1:2], None,
                                            ALU.mult).then_inc(misc_drained, 1)
                    dve.wait_ge(misc_drained, groups(group, it))
                    nc.vector.tensor_copy(wv_hi[:, :], wv[:, :]).then_inc(wv_split, 1)
                    dve.wait_ge(wv_split, 1)
                    nc.vector.tensor_tensor(wv_lo[:, :], wv[:, :], f(wv_hi[:, :]), ALU.subtract).then_inc(wv_split, 1)

            def emit(k, it):
                gb = drained_block(k)
                if gb is not None and BLOCKS[gb][0] == 1:
                    _, b, h = BLOCKS[gb]
                    dve.wait_ge(pv_done, chunks(gb, CPB - 1, it))
                    dve.wait_ge(misc_drained, groups(("r", b, h), it))
                    if b > 0:
                        dve.wait_ge(stored[h], 16 * b + 16 * it)
                    nc.vector.tensor_tensor(o_sb[:, cols(h)], accum[:, :], r_rows[:, :],
                                            ALU.mult).then_inc(accum_drained, 1)
                    dve.wait_ge(accum_drained, blocks(gb, it))
                    dve.wait_ge(misc_drained, groups(("f", b, h), it))
                    nc.vector.tensor_tensor(o_sb[:, cols(h)], o_sb[:, cols(h)], f_part[:, cols(h)],
                                            ALU.add).then_inc(out_ready, 1)
                gb = summed_block(k)
                if gb is not None:
                    dve.wait_ge(probs_ready, units(TPB * gb + TPB - 1, it))
                    nc.vector.reciprocal(r_inv[:, slot(gb), :], row_sum[:, slot(gb), :]).then_inc(r_inv_ready, 1)
                if 0 <= k - 2 < UNITS:
                    unit_lo(k - 2, it)
                for n, group in enumerate(SCHEDULE[k][0]):
                    if group[0] == "setup":
                        late_setup()
                    small(group, it)
                if 0 <= k < UNITS:
                    unit_max(k, it)
                for group in SCHEDULE[k][1]:
                    small(group, it)
            steps(dve, emit)

        @block.gpsimd
        def _(pool):
            nc.gpsimd.memset(zero[:, :], 0.0).then_inc(zero_ready, 1)
            nc.gpsimd.memset(ident[:, :], 0.0).then_inc(ident_ready, 1)
            pool.wait_ge(zero_ready, 1)

            def round_to(hi, full):
                return nc.gpsimd.tensor_tensor(hi, full, zero[:, :].broadcast_to([P, full.shape[1]]), ALU.add)

            def split_x(b, it):
                pool.wait_ge(x_loaded, 16 * b + 16 * it)
                pool.wait_ge(misc_ready, groups(("g", b - 1, 1), it))
                round_to(x_hi[:, :], x_raw[:, :]).then_inc(x_split, 1)
                pool.wait_ge(x_split, 2 * b + 1 + 2 * it)
                nc.gpsimd.tensor_tensor(x_lo[:, :], x_raw[:, :], f(x_hi[:, :]), ALU.subtract).then_inc(x_split, 1)

            def parts(full, hi, lo, done, count):
                round_to(hi, full).then_inc(done, 1)
                pool.wait_ge(done, count - 1)
                nc.gpsimd.tensor_tensor(lo, full, f(hi), ALU.subtract).then_inc(done, 1)

            def small(group, it):
                kind, b, h = group
                if kind not in ("theta", "phi", "g", "v", "y", "z"):
                    return
                pool.wait_ge(misc_drained, groups(group, it))
                if kind in ("theta", "phi"):
                    hi, lo = (theta_hi, theta_lo) if kind == "theta" else (phi_hi, phi_lo)
                    parts(proj_full[:, h, :], hi[:, cols(h)], lo[:, cols(h)], proj_split, projection(kind, b, h, it))
                    return
                if kind == "g":
                    if b > 0:
                        pool.wait_ge(pv_done, chunks(block_index(0, b - 1, 1), CPB - 1, it))
                    parts(g_full[:, :], g_hi[:, cols(h)], g_lo[:, cols(h)], g_split, halves(b, h, it, 2))
                elif kind == "v":
                    if b > 0:
                        last = (0, b, 1) if b == B - 1 else (1, b - 1, 1)
                        pool.wait_ge(pv_done, chunks(block_index(*last), CPB - 1, it))
                    hi, lo = v_of(b)
                    parts(v_full[:, :], hi[:, cols(h)], lo[:, cols(h)], v_split, halves(b, h, it, 2))
                elif kind == "y":
                    if 2 * b + h:
                        last = ("z", b, 0) if h else ("z", b - 1, 1)
                        pool.wait_ge(misc_ready, groups(last, it))
                    parts(y_full[:, :], y_hi[:, :], y_lo[:, :], y_split, halves(b, h, it, 2))
                else:
                    if b > 0:
                        last = ("f", b - 1, 1) if h else ("v", b - 1, 0)
                        pool.wait_ge(misc_ready, groups(last, it))
                    parts(z_full[:, :], z_hi[:, cols(h)], z_lo[:, cols(h)], z_split, halves(b, h, it, 2))

            def emit(k, it):
                if k in SPLIT_X:
                    split_x(SPLIT_X[k], it)
                gb = summed_block(k - 1)
                if gb is not None and BLOCKS[gb][0] == 1:
                    _, b, h = BLOCKS[gb]
                    n = out_count(gb, 0)
                    pool.wait_ge(r_inv_ready, blocks(gb, it))
                    if n > 1 or not isinstance(it, int):
                        last = ORDER["r", b, 0] if h else ORDER["r", b - 1, 1] if b else ORDER["r", b, 1] - GROUPS_PER_PERIOD
                        pool.wait_ge(misc_ready, last + 1 + GROUPS_PER_PERIOD * it)
                    round_to(r_hi[:, :], r_inv[:, slot(gb), :]).then_inc(r_split, 1)
                    pool.wait_ge(r_split, 2 * n - 1 + 4 * it)
                    nc.gpsimd.tensor_tensor(r_lo[:, :], r_inv[:, slot(gb), :], f(r_hi[:, :]), ALU.subtract).then_inc(r_split, 1)
                    pool.wait_ge(r_split, 2 * n + 4 * it)
                    eye = ident[:, :].unsqueeze(1).broadcast_to([P, TPB, P])
                    for diag, r in ((diag_hi, f(r_hi[:, :])), (diag_lo, r_lo[:, :])):
                        nc.gpsimd.tensor_tensor(diag[:, :].rearrange("p (n q) -> p n q", n=TPB), eye,
                                                r.unsqueeze(2).broadcast_to([P, TPB, P]), ALU.mult).then_inc(diag_ready, 1)
                for group in SCHEDULE[k][0] + SCHEDULE[k][1]:
                    small(group, it)
            pool.wait_ge(ident_ready, 1)
            nc.gpsimd.affine_select(out=ident[:, :], in_=ident[:, :], compare_op=ALU.not_equal, fill=1.0, base=0,
                                    pattern=[[-1, P]], channel_multiplier=1).then_inc(ident_ready, 1)
            rest = slice(2 * P, SPLIT_COLS)
            pool.wait_ge(rest_loaded, 16)
            nc.gpsimd.tensor_copy(w_hi[:, rest], w_all[:, rest]).then_inc(rest_split, 1)
            pool.wait_ge(rest_split, 1)
            nc.gpsimd.tensor_tensor(w_lo[:, rest], w_all[:, rest], f(w_hi[:, rest]), ALU.subtract).then_inc(rest_split, 1)
            pool.wait_ge(small_loaded, 64)
            nc.gpsimd.tensor_scalar(keep[:, 0:1], gate[:, 0:1], -1.0, 1.0, ALU.mult, ALU.add).then_inc(keep_made, 1)
            nc.gpsimd.tensor_tensor(keep[:, 1:2], gate[:, 0:1], col[:, 2:3], ALU.mult).then_inc(keep_made, 1)
            steps(pool, emit)


def kernel(x, L0_conv_theta_w, L0_conv_theta_b, L0_conv_phi_w, L0_conv_phi_b, L0_conv_g_w, L0_conv_g_b,
           L0_conv_wz_w, L0_conv_wz_b, L0_conv_w, L1_conv_Wq, L1_conv_bq, L1_conv_Wk, L1_conv_bk, L1_conv_Wv,
           L1_conv_bv, L1_conv_gamma, L1_conv_Wf, L1_conv_bf):
    import numpy as np
    import concourse.bacc as bacc
    from concourse.bass_utils import run_bass_kernel_spmd

    def a(v):
        return np.asarray(v)

    f1, f2 = a(L1_conv_Wf)[:, :C], a(L1_conv_Wf)[:, C:]
    qk = np.zeros((P, 2), np.float32)
    for n in range(3):
        qk[ROW * n:ROW * n + CK, 0] = a(L1_conv_bq)
        qk[ROW * n:ROW * n + CK, 1] = a(L1_conv_bk)
    arrays = {
        "x": np.ascontiguousarray(a(x).reshape(B, C, N)),
        "weights_t": np.ascontiguousarray(np.concatenate(
            [a(L0_conv_theta_w).T, a(L0_conv_phi_w).T, a(L0_conv_g_w).T, a(L0_conv_wz_w).T, f2.T, f1.T,
             a(L1_conv_Wv), a(L1_conv_Wq).T, a(L1_conv_Wk).T], axis=1)),
        "columns": np.ascontiguousarray(np.stack(
            [a(L0_conv_theta_b), a(L0_conv_phi_b), a(L0_conv_wz_b), a(L1_conv_bv), a(L1_conv_bf)], axis=1)),
        "qk_bias": qk,
        "g_bias": np.ascontiguousarray(a(L0_conv_g_b)),
        "gates": np.stack([a(L0_conv_w), a(L1_conv_gamma)]),
    }
    nc = bacc.Bacc("TRN2", target_bir_lowering=False, num_devices=1)
    args = [nc.dram_tensor(f"{name}_dram", v.shape, mybir.dt.from_np(v.dtype), kind="ExternalInput").ap()
            for name, v in arrays.items()]
    out = nc.dram_tensor("out_dram", (B, C, N), mybir.dt.float32, kind="ExternalOutput").ap()
    build(nc, *args, out)
    r = run_bass_kernel_spmd(nc, [{f"{name}_dram": v for name, v in arrays.items()}], core_ids=[0])
    return r.results[0]["out_dram"].reshape(B, C, 32, 32)
```

```python
from contextlib import ExitStack

import concourse.bass as bass
from concourse import mybir

B, C, N, CK = 8, 128, 1024, 16
P = 128
HALF = N // 2
TPB = HALF // P
KT = N // P
CPB = 4
ROW = 32
KROWS = 3 * ROW

BLOCKS = []
for _i in range(B + 2):
    if _i < B:
        BLOCKS.append((0, _i, 0))
    _between = [(1, _i - 2, 1)] if 0 <= _i - 2 else []
    _second = [(0, _i, 1)] if _i < B else []
    BLOCKS += _second + _between if _i == B - 1 else _between + _second
    if 0 <= _i - 1 < B:
        BLOCKS.append((1, _i - 1, 0))
UNITS = TPB * len(BLOCKS)
PERIOD = 16
LOOP_FROM, LOOP_TRIPS = 20, 5
LOOP_TO = LOOP_FROM + PERIOD * LOOP_TRIPS
LAST_STEP = UNITS + 5


def block_index(layer, b, h):
    return BLOCKS.index((layer, b, h))


def _schedule():
    at = {k: ([], []) for k in range(LAST_STEP)}

    def put(k, when, *groups):
        at[k][when].extend(groups)

    for n in range(4):
        put(n, 1, ("g", 0, n))
    put(5, 0, ("theta", 1, 0))
    put(5, 1, ("theta", 1, 1))
    put(6, 1, ("phi", 1, 0))
    put(7, 0, ("phi", 1, 1))
    put(8, 0, ("y", 0, 0))
    put(7, 1, ("g", 1, 0))
    put(8, 1, ("g", 1, 1))
    put(9, 0, ("g", 1, 2))
    put(9, 1, ("g", 1, 3))
    put(10, 0, ("z", 0, 0))
    put(10, 1, ("setup", 0, 0))
    put(11, 1, ("qk", 0, 0))
    put(12, 0, ("y", 0, 1))
    put(13, 0, ("z", 0, 1))
    put(14, 1, ("qk", 0, 1))
    put(15, 1, ("f", 0, 0))
    put(16, 0, ("theta", 2, 0))
    put(16, 1, ("v", 0, 0))
    put(17, 0, ("theta", 2, 1))
    put(17, 1, ("v", 0, 1))
    put(18, 0, ("phi", 2, 0))
    put(18, 1, ("v", 0, 2))
    put(19, 0, ("phi", 2, 1))
    put(19, 1, ("v", 0, 3))
    for i in range(2, B):
        k = LOOP_FROM + PERIOD * (i - 2)
        put(k, 0, ("y", i - 1, 0))
        put(k, 1, ("f", i - 2, 1))
        put(k + 1, 0, ("g", i, 0))
        put(k + 1, 1, ("z", i - 1, 0))
        put(k + 2, 0, ("g", i, 1))
        put(k + 2, 1, ("y", i - 1, 1))
        put(k + 3, 0, ("g", i, 2))
        put(k + 3, 1, ("g", i, 3))
        put(k + 4, 1, ("z", i - 1, 1))
        put(k + 5, 0, ("r", i - 2, 0))
        if i == B - 1:
            continue
        put(k + 6, 1, ("f", i - 1, 0))
        put(k + 7, 1, ("qk", i - 1, 0))
        put(k + 9, 1, ("qk", i - 1, 1))
        put(k + 11, 0, ("theta", i + 1, 0))
        put(k + 11, 1, ("r", i - 2, 1))
        put(k + 12, 0, ("theta", i + 1, 1))
        put(k + 13, 0, ("phi", i + 1, 0))
        put(k + 14, 0, ("phi", i + 1, 1))
        put(k + 8, 1, ("v", i - 1, 0))
        put(k + 10, 1, ("v", i - 1, 1))
        put(k + 14, 1, ("v", i - 1, 2))
        put(k + 15, 1, ("v", i - 1, 3))
    t = LOOP_FROM + PERIOD * (B - 3)
    put(t + 6, 1, ("f", B - 2, 0))
    put(t + 7, 1, ("qk", B - 2, 0))
    put(t + 8, 1, ("qk", B - 2, 1))
    put(t + 10, 1, ("y", B - 1, 0))
    put(t + 11, 0, ("v", B - 2, 0))
    put(t + 11, 1, ("v", B - 2, 1))
    put(t + 12, 0, ("z", B - 1, 0))
    put(t + 12, 1, ("v", B - 2, 2))
    put(t + 13, 0, ("f", B - 2, 1))
    put(t + 13, 1, ("v", B - 2, 3))
    put(t + 14, 1, ("y", B - 1, 1))
    put(t + 15, 1, ("qk", B - 1, 0))
    put(t + 16, 1, ("r", B - 3, 1))
    put(t + 17, 0, ("z", B - 1, 1))
    put(t + 17, 1, ("f", B - 1, 0))
    put(t + 18, 1, ("qk", B - 1, 1))
    put(t + 19, 1, ("r", B - 2, 0))
    for n in range(4):
        put(t + 20 + n, 1, ("v", B - 1, n))
    put(t + 24, 1, ("r", B - 2, 1))
    put(t + 25, 1, ("f", B - 1, 1))
    put(t + 27, 1, ("r", B - 1, 0))
    put(t + 30, 1, ("r", B - 1, 1))
    return at


SCHEDULE = _schedule()
ORDER = {}
for _k in range(LAST_STEP):
    for _g in SCHEDULE[_k][0] + SCHEDULE[_k][1]:
        ORDER[_g] = len(ORDER)
LOOP_GROUPS = sum(len(SCHEDULE[k][0] + SCHEDULE[k][1]) for k in range(LOOP_FROM))
GROUPS_PER_PERIOD = sum(len(SCHEDULE[k][0] + SCHEDULE[k][1]) for k in range(LOOP_FROM, LOOP_FROM + PERIOD))

HURRIED = {0: (6, 6, 7, 7), 1: (10, 10, 11, 11), 30: (126, 126, 127, 127), 31: (128, 128, 130, 131)}
VALUE_STEPS = [HURRIED.get(gb, tuple(TPB * gb + 6 + c for c in range(CPB))) for gb in range(len(BLOCKS))]

SPLIT_V = {k: (b, n // 2) for k in range(LAST_STEP) for kind, b, n in SCHEDULE[k][0] + SCHEDULE[k][1]
           if kind == "v" and n % 2 == 1 and not (n == 1 and LOOP_FROM <= k < LOOP_TO)}
SPLIT_V.update({LOOP_FROM + PERIOD * i + 14: (i + 1, 0) for i in range(LOOP_TRIPS)})

SPLIT_X = {3: 1, 14: 2, **{LOOP_FROM + PERIOD * (i - 2) + 9: i + 1 for i in range(2, B - 1)}}
KEEP_X = {0: 0, 5: 1, **{LOOP_FROM + PERIOD * (i - 2) + 5: i for i in range(2, B)}}
LOAD_X = {0: 1, 6: 2, **{LOOP_FROM + PERIOD * (i - 2) + 7: i + 1 for i in range(2, B - 1)}}

WARM_UP = 9

W_THETA, W_PHI, W_G, W_Z, W_F2, W_F1, W_V, W_Q = range(0, 8 * P, P)
W_K = W_Q + CK
W_COLS = 7 * P + 2 * CK
SPLIT_COLS = 5 * P


def build(nc, x, weights_t, columns, qk_bias, g_bias, gates, out):
    f32, f32r = mybir.dt.float32, mybir.dt.float32r
    ALU, ACT, AX = mybir.AluOpType, mybir.ActivationFunctionType, mybir.AxisListType

    with ExitStack() as ctx:
        def sb(name, shape, dt=f32):
            return ctx.enter_context(nc.sbuf_tensor(name, shape, dt))

        def sem(name):
            return ctx.enter_context(nc.semaphore(name))

        w_all = sb("w_all", [P, W_COLS])
        w_parts = sb("w_parts", [P, 2, SPLIT_COLS], f32r)
        w_hi, w_lo = w_parts[:, 0, :], w_parts[:, 1, :]
        wqk = sb("wqk", [P, 4, ROW])
        wqk_hi = sb("wqk_hi", [P, P], f32r)
        wqk_lo = sb("wqk_lo", [P, P], f32r)
        wv = sb("wv", [P, P])
        wv_parts = sb("wv_parts", [P, 2, P], f32r)
        f_bias = sb("f_bias", [P, 1])
        g_bias_rows = sb("g_bias_rows", [P, P])
        col = sb("col", [P, 5])
        qk_b = sb("qk_b", [P, 2])
        gate = sb("gate", [P, 2])
        keep = sb("keep", [P, 2])
        ident = sb("ident", [P, P])
        ones = sb("ones", [P, P])
        ones_r = sb("ones_r", [P, P], f32r)
        zero = sb("zero", [P, 1])
        warm = sb("warm", [P, 1])

        x_raw = sb("x_raw", [P, N])
        x_hi = sb("x_hi", [P, N], f32r)
        x_lo = sb("x_lo", [P, N], f32r)
        x_keep_0 = sb("x_keep_0", [P, N])
        x_keep = sb("x_keep", [P, N])
        theta_hi = sb("theta_hi", [P, N], f32r)
        theta_lo = sb("theta_lo", [P, N], f32r)
        phi_hi = sb("phi_hi", [P, N], f32r)
        phi_lo = sb("phi_lo", [P, N], f32r)
        proj_full = sb("proj_full", [P, 2, HALF])
        values_full = sb("values_full", [P, N])
        g_hi = sb("g_hi", [P, N], f32r)
        g_lo = sb("g_lo", [P, N], f32r)
        v_hi = sb("v_hi", [P, N], f32r)
        v_lo = sb("v_lo", [P, N], f32r)
        q_op = sb("q_op", [KROWS, N], f32r)
        k_op = sb("k_op", [KROWS, N], f32r)
        probs = sb("probs", [P, 2, N])
        pt_hi = sb("pt_hi", [P, 2, KT, HALF], f32r)
        pt_lo = sb("pt_lo", [P, 2, KT, HALF], f32r)
        neg_max = sb("neg_max", [P, 4])
        row_sum = sb("row_sum", [P, 4, TPB])
        r_inv = sb("r_inv", [P, 4, TPB])
        r_hi = sb("r_hi", [P, TPB], f32r)
        r_lo = sb("r_lo", [P, TPB])
        diag_hi = sb("diag_hi", [P, HALF], f32r)
        diag_lo = sb("diag_lo", [P, HALF], f32r)
        r_rows = sb("r_rows", [P, HALF])
        ut = sb("ut", [P, 2, HALF])
        y_full = sb("y_full", [P, HALF])
        y_hi = sb("y_hi", [P, HALF], f32r)
        y_lo = sb("y_lo", [P, HALF], f32r)
        z_full = sb("z_full", [P, HALF])
        z_hi = sb("z_hi", [P, N], f32r)
        z_lo = sb("z_lo", [P, N], f32r)
        f_part = sb("f_part", [P, N])
        o_sb = sb("o_sb", [P, N])
        g_hi_0 = sb("g_hi_0", [P, N], f32r)
        g_lo_0 = sb("g_lo_0", [P, N], f32r)

        def theta_of(b):
            return (v_hi, v_lo) if b == 0 else (theta_hi, theta_lo)

        def phi_of(b):
            return (z_hi, z_lo) if b == 0 else (phi_hi, phi_lo)

        def g_of(b):
            return (g_hi_0, g_lo_0) if b == 0 else (g_hi, g_lo)

        def q_of(b):
            return {B - 2: theta_lo, B - 1: theta_hi}.get(b, q_op)

        def k_of(b):
            return {B - 2: phi_lo, B - 1: phi_hi}.get(b, k_op)

        def v_of(b):
            return {B - 2: (x_hi, x_lo), B - 1: (g_hi, g_lo)}.get(b, (v_hi, v_lo))

        def f_of(b):
            return x_keep_0 if b == B - 2 else f_part

        scores = ctx.enter_context(nc.psum_tensor("scores", [P, 2, N], f32))
        trans = ctx.enter_context(nc.psum_tensor("trans", [P, N], f32))
        accum = ctx.enter_context(nc.psum_tensor("accum", [P, HALF], f32))
        misc = ctx.enter_context(nc.psum_tensor("misc", [P, HALF], f32))

        weights_loaded = sem("weights_loaded")
        rest_loaded = sem("rest_loaded")
        small_loaded = sem("small_loaded")
        x_loaded = sem("x_loaded")
        ident_ready = sem("ident_ready")
        consts_ready = sem("consts_ready")
        zero_ready = sem("zero_ready")
        w_split = sem("w_split")
        rest_split = sem("rest_split")
        wqk_made = sem("wqk_made")
        wqk_split = sem("wqk_split")
        setup_done = sem("setup_done")
        wv_split = sem("wv_split")
        x_split = sem("x_split")
        x_kept = sem("x_kept")
        scores_ready = sem("scores_ready")
        max_ready = sem("max_ready")
        probs_ready = sem("probs_ready")
        trans_ready = sem("trans_ready")
        pt_hi_ready = sem("pt_hi_ready")
        pt_lo_ready = sem("pt_lo_ready")
        pv_done = sem("pv_done")
        accum_drained = sem("accum_drained")
        r_inv_ready = sem("r_inv_ready")
        misc_ready = sem("misc_ready")
        misc_drained = sem("misc_drained")
        qk_hi_ready = sem("qk_hi_ready")
        q_lo_ready = sem("q_lo_ready")
        k_copied = sem("k_copied")
        proj_split = sem("proj_split")
        first_ready = sem("first_ready")
        first_hi = sem("first_hi")
        x_first = [sem("x_first_0"), sem("x_first_1")]
        x_first_hi = sem("x_first_hi")
        r_split = sem("r_split")
        keep_made = sem("keep_made")
        diag_ready = sem("diag_ready")
        g_biased = sem("g_biased")
        v_copied = sem("v_copied")
        g_split = sem("g_split")
        v_split = sem("v_split")
        y_split = sem("y_split")
        z_split = sem("z_split")
        last_scaled = sem("last_scaled")
        out_ready = sem("out_ready")
        stored = [sem("stored_0"), sem("stored_1")]

        def units(k, it):
            return k + 1 + PERIOD * it

        def banks(k, bank, it):
            return 2 * k + bank + 1 + 2 * PERIOD * it

        def blocks(gb, it):
            return gb + 1 + (PERIOD // TPB) * it

        def chunks(gb, c, it):
            return CPB * gb + c + 1 + PERIOD * it

        def groups(group, it):
            n = ORDER[group]
            if not isinstance(it, int) and n < LOOP_GROUPS:
                kind, b, h = group
                n = max(n, ORDER[kind, b + 1, h] - GROUPS_PER_PERIOD)
            return n + 1 + GROUPS_PER_PERIOD * it

        def halves(b, h, it, each=1):
            return each * (2 * b + h + 1) + 2 * each * it

        def projection(kind, b, h, it):
            return 8 * b + 4 * (kind == "phi") + 2 * h + 2 + 8 * it

        def out_count(gb, it):
            return sum(1 for n in range(gb + 1) if BLOCKS[n][0] == 1) + 2 * it

        def cols(h):
            return slice(h * HALF, (h + 1) * HALF)

        def f(ap):
            return ap.bitcast(f32)

        def steps(engine, emit):
            for k in range(LOOP_FROM):
                emit(k, 0)
            with engine.Fori(0, LOOP_TRIPS) as it:
                for k in range(LOOP_FROM, LOOP_FROM + PERIOD):
                    emit(k, it)
            for k in range(LOOP_TO, LAST_STEP):
                emit(k, 0)

        def slot(gb):
            layer, _, h = BLOCKS[gb]
            return 2 * layer + h

        def last_of_slot(gb):
            layer, b, h = BLOCKS[gb]
            return block_index(layer, b - 1, h) if b else gb - PERIOD // TPB

        def last_result(pair):
            return scores[:, 0, pair * HALF:pair * HALF + 2 * P]

        def last_cols(pair):
            return slice(HALF + pair * 2 * P, HALF + (pair + 1) * 2 * P)

        def drained_block(k):
            ended = [gb for gb in range(len(BLOCKS)) if VALUE_STEPS[gb][-1] == k - 1]
            return ended[0] if ended else None

        def quarter_free(engine, kind, b, h, it):
            if kind == "g" and b == 1:
                engine.wait_ge(g_split, halves(0, h, it, 2))
            elif kind == "g" and b > 1:
                engine.wait_ge(v_split, halves(b - 2, h, it, 2))
            elif kind == "v" and b < B - 1:
                engine.wait_ge(g_split, halves(b + 1, h, it, 2))
            elif kind == "v":
                engine.wait_ge(v_split, halves(b - 1, h, it, 2))

        def value_quarter(quarter):
            full = values_full[:, :].rearrange("p (q n c) -> p q n c", q=4, n=2)
            main, cross = (misc[:, :].rearrange("p (n s c) -> p n s c", n=2, s=2)[:, :, s, :] for s in (0, 1))
            return full[:, quarter, :, :], main, cross

        def summed_block(k):
            gb, off = divmod(k - 5, TPB)
            return gb if off == 0 and 0 <= gb < len(BLOCKS) else None

        block = ctx.enter_context(nc.Block())

        @block.sync
        def _(sp):
            for h in range(2):
                sp.dma_start(x_raw[:, cols(h)], x[0, :, cols(h)]).then_inc(x_first[h], 16)
            sp.dma_start(col[:, :], columns).then_inc(small_loaded, 16)
            sp.dma_start(qk_b[:, :], qk_bias).then_inc(small_loaded, 16)
            sp.dma_start(gate[:, :], gates.partition_broadcast(P)).then_inc(small_loaded, 16)
            sp.dma_start(g_bias_rows[:, :], g_bias.partition_broadcast(P)).then_inc(small_loaded, 16)
            sp.dma_start(w_all[:, 2 * P:W_COLS], weights_t[:, 2 * P:W_COLS]).then_inc(rest_loaded, 16)

            def emit(k, it):
                if k in LOAD_X:
                    b = LOAD_X[k]
                    sp.wait_ge(x_kept, b + it)
                    sp.dma_start(x_raw[:, :], x[b + it]).then_inc(x_loaded, 16)
                gb = drained_block(k)
                if gb is not None and BLOCKS[gb][0] == 1:
                    _, b, h = BLOCKS[gb]
                    sp.wait_ge(out_ready, out_count(gb, it))
                    if gb < len(BLOCKS) - 1:
                        sp.dma_start(out[b + it, :, cols(h)], o_sb[:, cols(h)]).then_inc(stored[h], 16)
                    else:
                        sp.dma_start(out[b, :, last_cols(0)], o_sb[:, last_cols(0)]).then_inc(stored[h], 16)
                        sp.wait_ge(out_ready, out_count(gb, it) + 1)
                        sp.dma_start(out[b, :, last_cols(1)], o_sb[:, last_cols(1)]).then_inc(stored[h], 16)
            steps(sp, emit)
            sp.wait_ge(stored[0], 16 * B)
            sp.wait_ge(stored[1], 16 * (B + 1))

        @block.tensor
        def _(pe):
            def three(dst, hi_l, lo_l, hi_r, lo_r):
                nc.tensor.matmul(dst, hi_l, hi_r, start=True, stop=False)
                nc.tensor.matmul(dst, hi_l, lo_r, start=False, stop=False)
                return nc.tensor.matmul(dst, lo_l, hi_r, start=False, stop=True)

            def unit_scores(k, it):
                layer, b, h = BLOCKS[k // TPB]
                t = k % TPB
                if k >= 2:
                    pe.wait_ge(probs_ready, units(k - 2, it))
                if t == 0 and layer == 0:
                    pe.wait_ge(proj_split, projection("phi", b, 0, it))
                if t == 0 and layer == 1:
                    pe.wait_ge(misc_drained, groups(("qk", b, 1), it))
                    pe.wait_ge(q_lo_ready, halves(b, 1, it))
                    pe.wait_ge(k_copied, halves(b, 1, it))
                for half in range(2):
                    if t == 0 and layer == 0 and half == 1:
                        pe.wait_ge(proj_split, projection("phi", b, 1, it))
                    dst = scores[:, k % 2, cols(half)]
                    if layer == 0:
                        queries = slice(TPB * h + t, N, KT)
                        (t_hi, t_lo), (p_hi, p_lo) = theta_of(b), phi_of(b)
                        last = three(dst, t_hi[:, queries], t_lo[:, queries], p_hi[:, cols(half)], p_lo[:, cols(half)])
                    else:
                        q0 = h * HALF + t * P
                        last = nc.tensor.matmul(dst, q_of(b)[0:KROWS, q0:q0 + P], k_of(b)[0:KROWS, cols(half)],
                                                start=True, stop=True)
                last.then_inc(scores_ready, 1)

            def unit_transposes(k, it):
                pe.wait_ge(probs_ready, units(k, it))
                for bank in range(2):
                    if k >= 1:
                        pe.wait_ge(pt_lo_ready, banks(k - 1, bank, it))
                    for n in range(4 * bank, 4 * bank + 4):
                        last = nc.tensor.transpose(trans[:, n * P:(n + 1) * P], probs[:, k % 2, n * P:(n + 1) * P],
                                                   ident[:, :])
                    last.then_inc(trans_ready, 1)

            def value_chunk(gb, c, it):
                layer, b, h = BLOCKS[gb]
                hi, lo = g_of(b) if layer == 0 else v_of(b)
                last_block = gb == len(BLOCKS) - 1
                if c == 0:
                    if not last_block:
                        pe.wait_ge(pt_lo_ready, banks(TPB * gb + TPB - 1, 1, it))
                    pe.wait_ge(g_split if layer == 0 else v_split, halves(b, 1, it, 2))
                    if gb and not last_block:
                        pe.wait_ge(accum_drained, blocks(gb - 1, it))
                tiles, queries = range(2 * c, 2 * c + 2), slice(0, HALF)
                if last_block:
                    pair, part = divmod(c, 2)
                    pe.wait_ge(pt_lo_ready, banks(TPB * gb + 2 * pair + 1, part, it))
                    tiles, queries = range(4 * part, 4 * part + 4), slice(pair * 2 * P, (pair + 1) * 2 * P)
                dst = last_result(pair) if last_block else accum[:, :]
                for n in tiles:
                    tile = slice(n * P, (n + 1) * P)
                    p_hi, p_lo = pt_hi[:, gb % 2, n, queries], pt_lo[:, gb % 2, n, queries]
                    nc.tensor.matmul(dst, hi[:, tile], p_hi, start=(n == 0), stop=False)
                    nc.tensor.matmul(dst, hi[:, tile], p_lo, start=False, stop=False)
                    last = nc.tensor.matmul(dst, lo[:, tile], p_hi, start=False, stop=(n == KT - 1))
                last.then_inc(pv_done, 1)

            def small(group, it):
                kind, b, h = group
                if ORDER[group]:
                    pe.wait_ge(misc_drained, ORDER[group] + GROUPS_PER_PERIOD * it)
                if kind in ("theta", "phi"):
                    w0 = W_THETA if kind == "theta" else W_PHI
                    pe.wait_ge(x_split, 2 * (b + 1) + 2 * it)
                    last = three(misc[:, :], w_hi[:, w0:w0 + P], w_lo[:, w0:w0 + P], x_hi[:, cols(h)], x_lo[:, cols(h)])
                elif kind in ("g", "v"):
                    if kind == "g":
                        pe.wait_ge(x_split, 2 * (b + 1) + 2 * it)
                        m_hi, m_lo, w = x_hi, x_lo, w_parts[:, :, W_G:W_G + P]
                    else:
                        if (b, h) == (0, 0):
                            pe.wait_ge(wv_split, 2)
                        pe.wait_ge(z_split, halves(b, h // 2, it, 2))
                        m_hi, m_lo, w = z_hi, z_lo, wv_parts[:, :, :]
                    for n in range(2):
                        tile = slice((2 * h + n) * P, (2 * h + n + 1) * P)
                        c0 = 2 * n * P
                        nc.tensor.matmul(misc[:, c0:c0 + 2 * P], m_hi[:, tile], w, start=True, stop=False)
                        last = nc.tensor.matmul(misc[:, c0:c0 + P], m_lo[:, tile], w[:, 0, :], start=False, stop=True)
                elif kind == "y":
                    pe.wait_ge(accum_drained, blocks(block_index(0, b, h), it))
                    for n in range(4):
                        last = nc.tensor.transpose(misc[:, n * P:(n + 1) * P], ut[:, h, n * P:(n + 1) * P], ident[:, :])
                elif kind == "z":
                    pe.wait_ge(y_split, halves(b, h, it, 2))
                    last = three(misc[:, :], w_hi[:, W_Z:W_Z + P], w_lo[:, W_Z:W_Z + P], y_hi[:, :], y_lo[:, :])
                elif kind == "qk":
                    if (b, h) == (0, 0):
                        pe.wait_ge(wqk_split, 2)
                    pe.wait_ge(z_split, halves(b, h, it, 2))
                    last = three(misc[:, :], wqk_hi[:, :], wqk_lo[:, :], z_hi[:, cols(h)], z_lo[:, cols(h)])
                elif kind == "f":
                    last = three(misc[:, :], w_hi[:, W_F2:W_F2 + P], w_lo[:, W_F2:W_F2 + P],
                                 z_hi[:, cols(h)], z_lo[:, cols(h)])
                elif kind == "r":
                    pe.wait_ge(diag_ready, 2 * out_count(block_index(1, b, h), it))
                    nc.tensor.matmul(misc[:, :], ones_r[:, :], diag_hi[:, :], start=True, stop=False)
                    last = nc.tensor.matmul(misc[:, :], ones_r[:, :], diag_lo[:, :], start=False, stop=True)
                else:
                    pe.wait_ge(consts_ready, 3)
                    nc.tensor.matmul(misc[:, 0:P], w_all[:, W_V:W_V + P], w_all[:, W_F1:W_F1 + P], start=True, stop=True)
                    last = nc.tensor.matmul(misc[:, P:P + 1], w_all[:, W_F1:W_F1 + P], col[:, 3:4],
                                            start=True, stop=True)
                last.then_inc(misc_ready, 1)

            pe.wait_ge(consts_ready, 2)
            for _ in range(WARM_UP):
                nc.tensor.matmul(misc[:, :], ones_r[:, :], ones_r[:, :].unsqueeze(1).broadcast_to([P, 4, P]),
                                 start=True, stop=True)
            pe.wait_ge(w_split, 2)
            for h in range(2):
                pe.wait_ge(x_split, h + 1)
                for i, w0 in enumerate((W_THETA, W_PHI)):
                    three(scores[:, i, cols(h)], w_hi[:, w0:w0 + P], w_lo[:, w0:w0 + P],
                          x_hi[:, cols(h)], x_lo[:, cols(h)]).then_inc(first_ready, 1)

            def emit(k, it):
                if 0 <= k < UNITS:
                    unit_scores(k, it)
                if k == 0:
                    pe.wait_ge(rest_split, 2)
                    pe.wait_ge(ident_ready, 2)
                before, after = SCHEDULE[k]
                for group in before:
                    small(group, it)
                for gb in range(len(BLOCKS)):
                    for c in range(CPB):
                        if VALUE_STEPS[gb][c] == k:
                            value_chunk(gb, c, it)
                for group in after:
                    small(group, it)
                if 0 <= k - 1 < UNITS:
                    unit_transposes(k - 1, it)
            steps(pe, emit)

        @block.scalar
        def _(act):
            act.dma_start(w_all[:, 0:2 * P], weights_t[:, 0:2 * P]).then_inc(weights_loaded, 16)
            act.wait_ge(consts_ready, 1)
            nc.scalar.activation(warm[:, :], ones[:, 0:1], ACT.Exp)
            for h in range(2):
                act.wait_ge(x_first[h], 16)
                nc.scalar.activation(x_hi[:, cols(h)], x_raw[:, cols(h)], ACT.Copy).then_inc(x_first_hi, 1)
            act.wait_ge(small_loaded, 64)
            for n, (h, i) in enumerate(((0, 0), (0, 1), (1, 0), (1, 1))):
                act.wait_ge(first_ready, n + 1)
                hi, _ = theta_of(0) if i == 0 else phi_of(0)
                nc.scalar.activation(hi[:, cols(h)], scores[:, i, cols(h)], ACT.Identity,
                                     bias=col[:, i:i + 1]).then_inc(first_hi, 1)

            def unit_exp(k, it):
                gb, t = divmod(k, TPB)
                act.wait_ge(max_ready, units(k, it))
                if k >= 2:
                    act.wait_ge(trans_ready, banks(k - 2, 1, it))
                if t == 0 and gb >= 5:
                    act.wait_ge(r_inv_ready, blocks(last_of_slot(gb), it))
                nc.scalar.activation(probs[:, k % 2, :], scores[:, k % 2, :], ACT.Exp, bias=neg_max[:, k % 4:k % 4 + 1],
                                     accum_out=row_sum[:, slot(gb), t:t + 1]).then_inc(probs_ready, 1)

            def unit_hi(k, it):
                gb, t = divmod(k, TPB)
                for bank in range(2):
                    act.wait_ge(trans_ready, banks(k, bank, it))
                    if t == 0 and bank == 0 and gb >= 2:
                        act.wait_ge(pv_done, chunks(gb - 2, CPB - 1, it))
                    nc.scalar.activation(pt_hi[:, gb % 2, 4 * bank:4 * bank + 4, t * P:(t + 1) * P],
                                         trans[:, cols(bank)].rearrange("p (n q) -> p n q", n=4),
                                         ACT.Copy).then_inc(pt_hi_ready, 1)

            def small(group, it):
                kind, b, h = group
                if kind not in ("theta", "phi", "v", "qk", "f", "r"):
                    return
                act.wait_ge(misc_ready, groups(group, it))
                if kind == "v":
                    quarter, main, _ = value_quarter(h)
                    if h % 2 == 0:
                        quarter_free(act, kind, b, h // 2, it)
                    nc.scalar.activation(quarter, main, ACT.Copy).then_inc(v_copied, 1)
                    return
                if kind in ("theta", "phi"):
                    c = 0 if kind == "theta" else 1
                    if projection(kind, b, h, 0) > 4:
                        act.wait_ge(proj_split, projection(kind, b, h, it) - 4)
                    nc.scalar.activation(proj_full[:, h, :], misc[:, :], ACT.Identity,
                                         bias=col[:, c:c + 1]).then_inc(misc_drained, 1)
                elif kind == "qk":
                    q, k = q_of(b), k_of(b)
                    nc.scalar.activation(q[0:KROWS, cols(h)], misc[0:KROWS, :], ACT.Identity,
                                         bias=qk_b[0:KROWS, 0:1]).then_inc(qk_hi_ready, 1)
                    nc.scalar.activation(k[0:ROW, cols(h)], misc[KROWS:P, :], ACT.Identity,
                                         bias=qk_b[KROWS:P, 0:1]).then_inc(qk_hi_ready, 1)
                elif kind == "f":
                    if h == 1 and not isinstance(it, int):
                        act.wait_ge(v_split, halves(b, 0, it, 2))
                    elif b > 0 and b != B - 2:
                        last = (1, b - 2 if b == B - 1 else b - 1, h)
                        act.wait_ge(out_ready, out_count(block_index(*last), it))
                    if (b, h) == (0, 0):
                        act.wait_ge(setup_done, 1)
                    nc.scalar.activation(f_of(b)[:, cols(h)], misc[:, :], ACT.Identity,
                                         bias=f_bias[:, :]).then_inc(misc_drained, 1)
                else:
                    nc.scalar.activation(r_rows[:, :], misc[:, :], ACT.Copy).then_inc(misc_drained, 1)

            def keep_x(b, it):
                act.wait_ge(x_split, 2 * b + 2 + 2 * it)
                if b >= 2:
                    act.wait_ge(misc_drained, groups(("z", b - 1, 1), it))
                dst = x_keep_0 if b == 0 else x_keep
                nc.scalar.activation(dst[:, :], x_raw[:, :], ACT.Identity, scale=keep[:, 0:1],
                                     bias=keep[:, 1:2]).then_inc(x_kept, 1)

            def emit(k, it):
                gb = drained_block(k)
                if gb is not None and BLOCKS[gb][0] == 0:
                    _, b, h = BLOCKS[gb]
                    act.wait_ge(pv_done, chunks(gb, CPB - 1, it))
                    if b > 0:
                        act.wait_ge(misc_ready, groups(("y", b - 1, h), it))
                    nc.scalar.activation(ut[:, h, :], accum[:, :], ACT.Copy).then_inc(accum_drained, 1)
                if 0 <= k - 2 < UNITS:
                    unit_hi(k - 2, it)
                if 0 <= k - 1 < UNITS:
                    unit_exp(k - 1, it)
                for group in SCHEDULE[k][0] + SCHEDULE[k][1]:
                    small(group, it)
                if k in KEEP_X:
                    if k == 0:
                        act.wait_ge(keep_made, 2)
                    keep_x(KEEP_X[k], it)
            steps(act, emit)

        @block.vector
        def _(dve):
            nc.vector.memset(ones[:, :], 1.0).then_inc(consts_ready, 1)
            nc.vector.memset(ones_r[:, :].bitcast(f32), 1.0).then_inc(consts_ready, 1)
            nc.vector.memset(wqk[:, :, :], 0.0).then_inc(wqk_made, 1)
            dve.wait_ge(weights_loaded, 16)
            nc.vector.tensor_copy(w_hi[:, 0:2 * P], w_all[:, 0:2 * P]).then_inc(w_split, 1)
            dve.wait_ge(w_split, 1)
            nc.vector.tensor_tensor(w_lo[:, 0:2 * P], w_all[:, 0:2 * P], f(w_hi[:, 0:2 * P]),
                                    ALU.subtract).then_inc(w_split, 1)
            for h in range(2):
                dve.wait_ge(x_first_hi, h + 1)
                nc.vector.tensor_tensor(x_lo[:, cols(h)], x_raw[:, cols(h)], f(x_hi[:, cols(h)]),
                                        ALU.subtract).then_inc(x_split, 1)
            dve.wait_ge(small_loaded, 64)
            for n, (h, i) in enumerate(((0, 0), (0, 1), (1, 0), (1, 1))):
                dve.wait_ge(first_hi, n + 1)
                hi, lo = theta_of(0) if i == 0 else phi_of(0)
                nc.vector.scalar_tensor_tensor(lo[:, cols(h)], scores[:, i, cols(h)], col[:, i:i + 1], f(hi[:, cols(h)]),
                                               ALU.add, ALU.subtract).then_inc(proj_split, 2)

            def late_setup():
                dve.wait_ge(rest_loaded, 16)
                dve.wait_ge(consts_ready, 2)
                nc.vector.tensor_scalar(qk_b[0:KROWS, 0:1], qk_b[0:KROWS, 0:1], CK ** -0.5, None, ALU.mult).then_inc(consts_ready, 1)
                dve.wait_ge(wqk_made, 1)
                for n in range(4):
                    w0, scale = (W_Q, CK ** -0.5) if n < 3 else (W_K, 1.0)
                    nc.vector.tensor_scalar(wqk[:, n, 0:CK], w_all[:, w0:w0 + CK], scale, None,
                                            ALU.mult).then_inc(wqk_made, 1)
                dve.wait_ge(wqk_made, 5)
                flat = wqk[:, :, :].rearrange("p n c -> p (n c)")
                nc.vector.tensor_copy(wqk_hi[:, :], flat).then_inc(wqk_split, 1)
                dve.wait_ge(wqk_split, 1)
                nc.vector.tensor_tensor(wqk_lo[:, :], flat, f(wqk_hi[:, :]), ALU.subtract).then_inc(wqk_split, 1)

            def unit_max(k, it):
                dve.wait_ge(scores_ready, units(k, it))
                if k >= 4:
                    dve.wait_ge(probs_ready, units(k - 4, it))
                nc.vector.tensor_reduce(neg_max[:, k % 4:k % 4 + 1], scores[:, k % 2, :], AX.X, ALU.max,
                                        negate=True).then_inc(max_ready, 1)

            def unit_lo(k, it):
                gb, t = divmod(k, TPB)
                for bank in range(2):
                    dve.wait_ge(pt_hi_ready, banks(k, bank, it))
                    if t == 0 and bank == 0 and gb >= 2:
                        dve.wait_ge(pv_done, chunks(gb - 2, CPB - 1, it))
                    at = (slice(None), gb % 2, slice(4 * bank, 4 * bank + 4), slice(t * P, (t + 1) * P))
                    nc.vector.tensor_tensor(pt_lo[at], trans[:, cols(bank)].rearrange("p (n q) -> p n q", n=4),
                                            f(pt_hi[at]), ALU.subtract).then_inc(pt_lo_ready, 1)

            def small(group, it):
                kind, b, h = group
                if kind in ("theta", "phi", "f", "r"):
                    return
                if kind == "qk":
                    q, k = q_of(b), k_of(b)
                    two, three = slice(ROW, 2 * ROW), slice(2 * ROW, 3 * ROW)
                    dve.wait_ge(qk_hi_ready, halves(b, h, it, 2) - 1)
                    nc.vector.scalar_tensor_tensor(q[two, cols(h)], misc[two, :], qk_b[two, 0:1], f(q[two, cols(h)]),
                                                   ALU.add, ALU.subtract).then_inc(q_lo_ready, 1)
                    dve.wait_ge(qk_hi_ready, halves(b, h, it, 2))
                    nc.vector.scalar_tensor_tensor(k[three, cols(h)], misc[KROWS:P, :], qk_b[0:ROW, 1:2],
                                                   f(k[0:ROW, cols(h)]), ALU.add, ALU.subtract).then_inc(misc_drained, 1)
                    nc.vector.tensor_copy(k[two, cols(h)], f(k[0:ROW, cols(h)])).then_inc(k_copied, 1)
                    return
                dve.wait_ge(misc_ready, groups(group, it))
                four = misc[:, :].rearrange("p (n c) -> p n c", n=4)
                if kind in ("g", "v"):
                    quarter, main, cross = value_quarter(h)
                    if kind == "g":
                        if h % 2 == 0:
                            quarter_free(dve, kind, b, h // 2, it)
                        nc.vector.tensor_tensor(quarter, main, g_bias_rows[:, :].unsqueeze(1).broadcast_to([P, 2, P]),
                                                ALU.add).then_inc(g_biased, 1)
                        dve.wait_ge(g_biased, 4 * b + h + 1 + 4 * it)
                    else:
                        dve.wait_ge(v_copied, 4 * b + h + 1 + 4 * it)
                    nc.vector.tensor_tensor(quarter, cross, quarter, ALU.add).then_inc(misc_drained, 1)
                elif kind == "y":
                    if 2 * b + h:
                        dve.wait_ge(y_split, halves(b, h, it, 2) - 2)
                    gb = block_index(0, b, h)
                    dve.wait_ge(r_inv_ready, blocks(gb, it))
                    nc.vector.tensor_tensor(y_full[:, :].rearrange("p (n c) -> p n c", n=4), four,
                                            r_inv[:, slot(gb), :].unsqueeze(2).broadcast_to([P, 4, P]),
                                            ALU.mult).then_inc(misc_drained, 1)
                elif kind == "z":
                    if 2 * b + h:
                        dve.wait_ge(z_split, halves(b, h, it, 2) - 2)
                    dve.wait_ge(x_kept, b + 1 + it)
                    keep_of = x_keep_0 if b == 0 else x_keep
                    nc.vector.scalar_tensor_tensor(z_full[:, :], misc[:, :], gate[:, 0:1], keep_of[:, cols(h)],
                                                   ALU.mult, ALU.add).then_inc(misc_drained, 1)
                else:
                    nc.vector.scalar_tensor_tensor(f_bias[:, :], misc[:, P:P + 1], gate[:, 1:2], col[:, 4:5],
                                                   ALU.mult, ALU.add).then_inc(setup_done, 1)
                    nc.vector.tensor_scalar(wv[:, :], misc[:, 0:P], gate[:, 1:2], None,
                                            ALU.mult).then_inc(misc_drained, 1)
                    dve.wait_ge(misc_drained, groups(group, it))
                    nc.vector.tensor_copy(wv_parts[:, 0, :], wv[:, :]).then_inc(wv_split, 1)
                    dve.wait_ge(wv_split, 1)
                    nc.vector.tensor_tensor(wv_parts[:, 1, :], wv[:, :], f(wv_parts[:, 0, :]), ALU.subtract).then_inc(wv_split, 1)

            def emit(k, it):
                gb = drained_block(k)
                if gb is not None and BLOCKS[gb][0] == 1:
                    _, b, h = BLOCKS[gb]
                    dve.wait_ge(misc_drained, groups(("r", b, h), it))
                    if b > 0:
                        dve.wait_ge(stored[h], 16 * b + 16 * it)
                    if gb < len(BLOCKS) - 1:
                        dve.wait_ge(pv_done, chunks(gb, CPB - 1, it))
                        nc.vector.tensor_tensor(o_sb[:, cols(h)], accum[:, :], r_rows[:, :],
                                                ALU.mult).then_inc(accum_drained, 1)
                    else:
                        dve.wait_ge(misc_drained, groups(("f", b, h), it))
                        for pair in range(2):
                            dve.wait_ge(pv_done, chunks(gb, 2 * pair + 1, it))
                            at = last_cols(pair)
                            nc.vector.tensor_tensor(o_sb[:, at], last_result(pair), r_rows[:, at.start - HALF:at.stop - HALF],
                                                    ALU.mult).then_inc(last_scaled, 1)
                            dve.wait_ge(last_scaled, pair + 1)
                            nc.vector.tensor_tensor(o_sb[:, at], o_sb[:, at], f_of(b)[:, at],
                                                    ALU.add).then_inc(out_ready, 1)
                gb = summed_block(k)
                if gb is not None:
                    dve.wait_ge(probs_ready, units(TPB * gb + TPB - 1, it))
                    nc.vector.reciprocal(r_inv[:, slot(gb), :], row_sum[:, slot(gb), :]).then_inc(r_inv_ready, 1)
                if 0 <= k - 2 < UNITS:
                    unit_lo(k - 2, it)
                if k == 2:
                    late_setup()
                before, after = SCHEDULE[k]
                for group in before:
                    small(group, it)
                if 0 <= k < UNITS:
                    unit_max(k, it)
                for group in after:
                    small(group, it)
            steps(dve, emit)

        @block.gpsimd
        def _(pool):
            nc.gpsimd.memset(zero[:, :], 0.0).then_inc(zero_ready, 1)
            nc.gpsimd.memset(ident[:, :], 0.0).then_inc(ident_ready, 1)
            pool.wait_ge(zero_ready, 1)

            def round_to(hi, full):
                return nc.gpsimd.tensor_tensor(hi, full, zero[:, :].broadcast_to([P, full.shape[1]]), ALU.add)

            def split_x(b, it):
                pool.wait_ge(x_loaded, 16 * b + 16 * it)
                pool.wait_ge(misc_ready, groups(("g", b - 1, 3), it))
                round_to(x_hi[:, :], x_raw[:, :]).then_inc(x_split, 1)
                pool.wait_ge(x_split, 2 * b + 1 + 2 * it)
                nc.gpsimd.tensor_tensor(x_lo[:, :], x_raw[:, :], f(x_hi[:, :]), ALU.subtract).then_inc(x_split, 1)

            def parts(full, hi, lo, done, count):
                round_to(hi, full).then_inc(done, 1)
                pool.wait_ge(done, count - 1)
                nc.gpsimd.tensor_tensor(lo, full, f(hi), ALU.subtract).then_inc(done, 1)

            def small(group, it):
                kind, b, h = group
                if kind not in ("theta", "phi", "g", "y", "z"):
                    return
                if kind == "g":
                    if h % 2 == 0:
                        return
                    h = h // 2
                pool.wait_ge(misc_drained, groups(group, it))
                if kind in ("theta", "phi"):
                    hi, lo = (theta_hi, theta_lo) if kind == "theta" else (phi_hi, phi_lo)
                    parts(proj_full[:, h, :], hi[:, cols(h)], lo[:, cols(h)], proj_split, projection(kind, b, h, it))
                    return
                if kind == "g":
                    if b > 1:
                        pool.wait_ge(pv_done, chunks(block_index(0, b - 1, 1), CPB - 1, it))
                    hi, lo = g_of(b)
                    parts(values_full[:, cols(h)], hi[:, cols(h)], lo[:, cols(h)], g_split, halves(b, h, it, 2))
                elif kind == "y":
                    if 2 * b + h:
                        last = ("z", b, 0) if h else ("z", b - 1, 1)
                        pool.wait_ge(misc_ready, groups(last, it))
                    parts(y_full[:, :], y_hi[:, :], y_lo[:, :], y_split, halves(b, h, it, 2))
                else:
                    if b > 0:
                        readers = [(kind, b - 1, h) for kind in ("qk", "f")] + [("v", b - 1, 2 * h + 1)]
                        last = max(readers, key=ORDER.get)
                        pool.wait_ge(misc_ready, groups(last, it))
                    parts(z_full[:, :], z_hi[:, cols(h)], z_lo[:, cols(h)], z_split, halves(b, h, it, 2))

            def split_v(b, h, it):
                pool.wait_ge(misc_drained, groups(("v", b, 2 * h + 1), it))
                if b > 0 and b != B - 2:
                    last = (0, b, 1) if b == B - 1 else (1, b - 1, 1)
                    pool.wait_ge(pv_done, chunks(block_index(*last), CPB - 1, it))
                hi, lo = v_of(b)
                parts(values_full[:, cols(h)], hi[:, cols(h)], lo[:, cols(h)], v_split, halves(b, h, it, 2))

            def emit(k, it):
                if k in SPLIT_X:
                    split_x(SPLIT_X[k], it)
                gb = summed_block(k - 1)
                if gb is not None and BLOCKS[gb][0] == 1:
                    _, b, h = BLOCKS[gb]
                    n = out_count(gb, 0)
                    pool.wait_ge(r_inv_ready, blocks(gb, it))
                    if n > 1 or not isinstance(it, int):
                        last = ORDER["r", b, 0] if h else ORDER["r", b - 1, 1] if b else ORDER["r", b, 1] - GROUPS_PER_PERIOD
                        pool.wait_ge(misc_ready, last + 1 + GROUPS_PER_PERIOD * it)
                    round_to(r_hi[:, :], r_inv[:, slot(gb), :]).then_inc(r_split, 1)
                    pool.wait_ge(r_split, 2 * n - 1 + 4 * it)
                    nc.gpsimd.tensor_tensor(r_lo[:, :], r_inv[:, slot(gb), :], f(r_hi[:, :]), ALU.subtract).then_inc(r_split, 1)
                    pool.wait_ge(r_split, 2 * n + 4 * it)
                    eye = ident[:, :].unsqueeze(1).broadcast_to([P, TPB, P])
                    for diag, r in ((diag_hi, f(r_hi[:, :])), (diag_lo, r_lo[:, :])):
                        nc.gpsimd.tensor_tensor(diag[:, :].rearrange("p (n q) -> p n q", n=TPB), eye,
                                                r.unsqueeze(2).broadcast_to([P, TPB, P]), ALU.mult).then_inc(diag_ready, 1)
                for group in SCHEDULE[k][0] + SCHEDULE[k][1]:
                    small(group, it)
                gb = drained_block(k)
                if gb is not None and BLOCKS[gb][0] == 1 and gb < len(BLOCKS) - 1:
                    _, b, h = BLOCKS[gb]
                    pool.wait_ge(accum_drained, blocks(gb, it))
                    pool.wait_ge(misc_drained, groups(("f", b, h), it))
                    nc.gpsimd.tensor_tensor(o_sb[:, cols(h)], o_sb[:, cols(h)], f_of(b)[:, cols(h)],
                                            ALU.add).then_inc(out_ready, 1)
                if k in SPLIT_V:
                    split_v(*SPLIT_V[k], it)
            pool.wait_ge(ident_ready, 1)
            nc.gpsimd.affine_select(out=ident[:, :], in_=ident[:, :], compare_op=ALU.not_equal, fill=1.0, base=0,
                                    pattern=[[-1, P]], channel_multiplier=1).then_inc(ident_ready, 1)
            rest = slice(2 * P, SPLIT_COLS)
            pool.wait_ge(rest_loaded, 16)
            nc.gpsimd.tensor_copy(w_hi[:, rest], w_all[:, rest]).then_inc(rest_split, 1)
            pool.wait_ge(rest_split, 1)
            nc.gpsimd.tensor_tensor(w_lo[:, rest], w_all[:, rest], f(w_hi[:, rest]), ALU.subtract).then_inc(rest_split, 1)
            pool.wait_ge(small_loaded, 64)
            nc.gpsimd.tensor_scalar(keep[:, 0:1], gate[:, 0:1], -1.0, 1.0, ALU.mult, ALU.add).then_inc(keep_made, 1)
            nc.gpsimd.tensor_tensor(keep[:, 1:2], gate[:, 0:1], col[:, 2:3], ALU.mult).then_inc(keep_made, 1)
            steps(pool, emit)


def kernel(x, L0_conv_theta_w, L0_conv_theta_b, L0_conv_phi_w, L0_conv_phi_b, L0_conv_g_w, L0_conv_g_b,
           L0_conv_wz_w, L0_conv_wz_b, L0_conv_w, L1_conv_Wq, L1_conv_bq, L1_conv_Wk, L1_conv_bk, L1_conv_Wv,
           L1_conv_bv, L1_conv_gamma, L1_conv_Wf, L1_conv_bf):
    import numpy as np
    import concourse.bacc as bacc
    from concourse.bass_utils import run_bass_kernel_spmd

    def a(v):
        return np.asarray(v)

    f1, f2 = a(L1_conv_Wf)[:, :C], a(L1_conv_Wf)[:, C:]
    qk = np.zeros((P, 2), np.float32)
    for n in range(4):
        qk[ROW * n:ROW * n + CK, 0] = a(L1_conv_bq) if n < 3 else a(L1_conv_bk)
    qk[0:CK, 1] = a(L1_conv_bk)
    arrays = {
        "x": np.ascontiguousarray(a(x).reshape(B, C, N)),
        "weights_t": np.ascontiguousarray(np.concatenate(
            [a(L0_conv_theta_w).T, a(L0_conv_phi_w).T, a(L0_conv_g_w).T, a(L0_conv_wz_w).T, f2.T, f1.T,
             a(L1_conv_Wv), a(L1_conv_Wq).T, a(L1_conv_Wk).T], axis=1)),
        "columns": np.ascontiguousarray(np.stack(
            [a(L0_conv_theta_b), a(L0_conv_phi_b), a(L0_conv_wz_b), a(L1_conv_bv), a(L1_conv_bf)], axis=1)),
        "qk_bias": qk,
        "g_bias": np.ascontiguousarray(a(L0_conv_g_b)),
        "gates": np.stack([a(L0_conv_w), a(L1_conv_gamma)]),
    }
    nc = bacc.Bacc("TRN2", target_bir_lowering=False, num_devices=1)
    args = [nc.dram_tensor(f"{name}_dram", v.shape, mybir.dt.from_np(v.dtype), kind="ExternalInput").ap()
            for name, v in arrays.items()]
    out = nc.dram_tensor("out_dram", (B, C, N), mybir.dt.float32, kind="ExternalOutput").ap()
    build(nc, *args, out)
    r = run_bass_kernel_spmd(nc, [{f"{name}_dram": v for name, v in arrays.items()}], core_ids=[0])
    return r.results[0]["out_dram"].reshape(B, C, 32, 32)
```
